# Optimizing a Trainium2 kernel written in Bass

```python
import numpy as np
import jax
import jax.numpy as jnp

def _softmax(x, axis=-1):
    return jax.nn.softmax(x, axis=axis)

def _gelu(x):
    return jax.nn.gelu(x, approximate=True)

def _silu(x):
    return jax.nn.silu(x)

def _sigmoid(x):
    return jax.nn.sigmoid(x)

def _layernorm(x, axis=-1, eps=1e-05):
    m = jnp.mean(x, axis=axis, keepdims=True)
    v = jnp.var(x, axis=axis, keepdims=True)
    return (x - m) / jnp.sqrt(v + eps)

def _scatter_add(tgt, idx, src, axis=0):
    return tgt.at[idx].add(src)

def _segment_sum(src, seg, n):
    return jax.ops.segment_sum(src, seg, n)
kernel_name = 'mk_seq_postln_d1_jaxref_r8_5696b8'

def setup_inputs(seed: int=0):
    np.random.seed(seed)
    _w = jnp.asarray

    def _L0_attn_setup():
        import jax, jax.numpy as jnp
        import numpy as np
        D_MODEL = 128
        NUM_HEADS = 16
        D_K = D_MODEL // NUM_HEADS
        MAX_SEQ_LEN = 512
        THETA = 10000.0

        def _rope_tables(seq_len):
            pos = jnp.arange(seq_len, dtype=jnp.float32)
            pair = jnp.arange(D_K // 2, dtype=jnp.float32)
            rates = THETA ** (-(2.0 * pair) / D_K)
            angles = pos[:, None] * rates[None, :]
            return (jnp.cos(angles), jnp.sin(angles))

        def _apply_rope(x, cos, sin):
            x_even = x[..., 0::2]
            x_odd = x[..., 1::2]
            r_even = x_even * cos - x_odd * sin
            r_odd = x_even * sin + x_odd * cos
            out = jnp.stack([r_even, r_odd], axis=-1)
            return out.reshape(x.shape)
        key = jax.random.key(seed)
        ks = jax.random.split(key, 5)
        x = jax.random.normal(ks[0], (1, 512, D_MODEL), dtype=jnp.float32)
        Wq = jax.random.truncated_normal(ks[1], -2.0, 2.0, (D_MODEL, D_MODEL), dtype=jnp.float32) * D_MODEL ** (-0.5)
        Wk = jax.random.truncated_normal(ks[2], -2.0, 2.0, (D_MODEL, D_MODEL), dtype=jnp.float32) * D_MODEL ** (-0.5)
        Wv = jax.random.truncated_normal(ks[3], -2.0, 2.0, (D_MODEL, D_MODEL), dtype=jnp.float32) * D_MODEL ** (-0.5)
        Wo = jax.random.truncated_normal(ks[4], -2.0, 2.0, (D_MODEL, D_MODEL), dtype=jnp.float32) * D_MODEL ** (-0.5)
        return {'x': x, 'Wq': Wq, 'Wk': Wk, 'Wv': Wv, 'Wo': Wo}
    _L0_attn_in = _L0_attn_setup()

    def _L0_ffn_setup():
        import jax, jax.numpy as jnp
        import numpy as np
        B, SEQ, D, E, F = (4, 128, 128, 8, 512)
        CAPACITY = 2
        key = jax.random.key(seed)
        ks = jax.random.split(key, 8)
        x = jax.random.normal(ks[0], (B, SEQ, D), jnp.float32)
        gate_weight = jax.random.normal(ks[1], (E, D), jnp.float32) * 0.006
        W1 = jax.random.normal(ks[2], (E, D, F), jnp.float32) * (1.0 / np.sqrt(D))
        b1 = jnp.zeros((E, F), jnp.float32)
        W2 = jax.random.normal(ks[3], (E, F, D), jnp.float32) * (1.0 / np.sqrt(F))
        b2 = jnp.zeros((E, D), jnp.float32)
        Ws1 = jax.random.normal(ks[4], (D, F), jnp.float32) * (1.0 / np.sqrt(D))
        bs1 = jnp.zeros((F,), jnp.float32)
        Ws2 = jax.random.normal(ks[5], (F, D), jnp.float32) * (1.0 / np.sqrt(F))
        bs2 = jnp.zeros((D,), jnp.float32)
        return {'x': x, 'gate_weight': gate_weight, 'W1': W1, 'b1': b1, 'W2': W2, 'b2': b2, 'Ws1': Ws1, 'bs1': bs1, 'Ws2': Ws2, 'bs2': bs2}
    _L0_ffn_in = _L0_ffn_setup()
    _d = {'L0_attn_x': _L0_attn_in['x'], 'L0_attn_Wq': _L0_attn_in['Wq'], 'L0_attn_Wk': _L0_attn_in['Wk'], 'L0_attn_Wv': _L0_attn_in['Wv'], 'L0_attn_Wo': _L0_attn_in['Wo'], 'L0_ffn_gate_weight': _L0_ffn_in['gate_weight'], 'L0_ffn_W1': _L0_ffn_in['W1'], 'L0_ffn_b1': _L0_ffn_in['b1'], 'L0_ffn_W2': _L0_ffn_in['W2'], 'L0_ffn_b2': _L0_ffn_in['b2'], 'L0_ffn_Ws1': _L0_ffn_in['Ws1'], 'L0_ffn_bs1': _L0_ffn_in['bs1'], 'L0_ffn_Ws2': _L0_ffn_in['Ws2'], 'L0_ffn_bs2': _L0_ffn_in['bs2']}
    _x0 = _d['L0_attn_x']
    _d['L0_attn_x'] = jax.random.normal(jax.random.fold_in(jax.random.key(seed), 1), (8, 512, 128), dtype=_x0.dtype)
    del _x0
    return _d

def reference(L0_attn_x, L0_attn_Wq, L0_attn_Wk, L0_attn_Wv, L0_attn_Wo, L0_ffn_gate_weight, L0_ffn_W1, L0_ffn_b1, L0_ffn_W2, L0_ffn_b2, L0_ffn_Ws1, L0_ffn_bs1, L0_ffn_Ws2, L0_ffn_bs2):

    def _L0_attn_ref(x, Wq, Wk, Wv, Wo):
        import jax, jax.numpy as jnp
        import numpy as np
        D_MODEL = 128
        NUM_HEADS = 16
        D_K = D_MODEL // NUM_HEADS
        MAX_SEQ_LEN = 512
        THETA = 10000.0

        def _rope_tables(seq_len):
            pos = jnp.arange(seq_len, dtype=jnp.float32)
            pair = jnp.arange(D_K // 2, dtype=jnp.float32)
            rates = THETA ** (-(2.0 * pair) / D_K)
            angles = pos[:, None] * rates[None, :]
            return (jnp.cos(angles), jnp.sin(angles))

        def _apply_rope(x, cos, sin):
            x_even = x[..., 0::2]
            x_odd = x[..., 1::2]
            r_even = x_even * cos - x_odd * sin
            r_odd = x_even * sin + x_odd * cos
            out = jnp.stack([r_even, r_odd], axis=-1)
            return out.reshape(x.shape)
        b, s, _ = x.shape

        def split_heads(t):
            return t.reshape(b, s, NUM_HEADS, D_K).transpose(0, 2, 1, 3)
        q = split_heads(x @ Wq.T)
        k = split_heads(x @ Wk.T)
        v = split_heads(x @ Wv.T)
        cos, sin = _rope_tables(s)
        q = _apply_rope(q, cos, sin)
        k = _apply_rope(k, cos, sin)
        scores = jnp.einsum('bhqd,bhkd->bhqk', q, k) / jnp.sqrt(jnp.float32(D_K))
        causal = jnp.tril(jnp.ones((s, s), dtype=bool))
        scores = jnp.where(causal, scores, jnp.float32(-1000000000.0))
        probs = jax.nn.softmax(scores, axis=-1)
        attn = jnp.einsum('bhqk,bhkd->bhqd', probs, v)
        attn = attn.transpose(0, 2, 1, 3).reshape(b, s, D_MODEL)
        return attn @ Wo.T

    def _L0_ffn_ref(x, gate_weight, W1, b1, W2, b2, Ws1, bs1, Ws2, bs2):
        import jax, jax.numpy as jnp
        import numpy as np
        B, SEQ, D, E, F = (4, 128, 128, 8, 512)
        CAPACITY = 2
        Bb, s, Dd = x.shape
        Ee = gate_weight.shape[0]
        xf = x.reshape(-1, Dd)
        S = xf.shape[0]
        logits = xf @ gate_weight.T
        scores = jax.nn.softmax(logits, axis=-1).T
        k = S * CAPACITY
        vals, idx = jax.lax.top_k(scores.reshape(-1), k)
        eidx = idx // S
        tidx = idx % S
        gate = jnp.zeros((Ee, S), x.dtype).at[eidx, tidx].add(vals)
        h = jax.nn.gelu(jnp.einsum('sd,edf->esf', xf, W1) + b1[:, None, :], approximate=True)
        y = jnp.einsum('esf,efd->esd', h, W2) + b2[:, None, :]
        out = jnp.einsum('es,esd->sd', gate, y)
        shared = jax.nn.gelu(xf @ Ws1 + bs1, approximate=True) @ Ws2 + bs2
        out = out + shared
        return out.reshape(Bb, s, Dd)
    x = L0_attn_x
    x = _layernorm(x + _L0_attn_ref(x, L0_attn_Wq, L0_attn_Wk, L0_attn_Wv, L0_attn_Wo), axis=-1)
    x = _layernorm(x + _L0_ffn_ref(x, L0_ffn_gate_weight, L0_ffn_W1, L0_ffn_b1, L0_ffn_W2, L0_ffn_b2, L0_ffn_Ws1, L0_ffn_bs1, L0_ffn_Ws2, L0_ffn_bs2), axis=-1)
    return x

_drawn_inputs = setup_inputs


def setup_inputs(seed=0):
    import zlib

    import numpy as np

    out = dict(_drawn_inputs(seed))
    spreads = {'L0_ffn_b1': (0.0, 0.757),
     'L0_ffn_b2': (0.0, 0.516),
     'L0_ffn_bs1': (0.0, 0.1),
     'L0_ffn_bs2': (0.0, 0.1)}
    factors = {}
    for name, (base, spread) in spreads.items():
        noise = np.random.default_rng([zlib.crc32(name.encode()), seed]).standard_normal(out[name].shape)
        drawn = base * np.exp(spread * noise) if base else spread * noise
        out[name] = jnp.asarray(drawn.astype(out[name].dtype))
    for name, factor in factors.items():
        out[name] = (out[name] * factor).astype(out[name].dtype)
    return out
```

```python
from contextlib import ExitStack

import concourse.bass as bass
from concourse import mybir

ALU = mybir.AluOpType
ACT = mybir.ActivationFunctionType
AX = mybir.AxisListType
F32 = mybir.dt.float32
F32R = mybir.dt.float32r
BF16 = mybir.dt.bfloat16
U32 = mybir.dt.uint32
I32 = mybir.dt.int32

P = 128
NB = 8
S = 512
D = 128
NH = 16
DK = 8
NG = 4
NC = S // P
NE = 8
NX = NE + 1
F = 512
NF = F // P
TOK = NB * S
NCH = TOK // P
TOPK = 2 * TOK
EPS = 1e-5
SCALE = DK ** -0.5
NEG = -1e30
SEG = {0: 0, 1: 512, 3: 896, 2: 1024}
SEGW = 1280
BSTEPS = [(0,), (1, 3), (2,)]
Q_AT, QS_AT, K_AT, KS_AT, M0_AT, V_AT = (0, 0), (0, 1), (1, 0), (1, 1), (2, 0), (4, 0)
OT_AT, AT_AT, WO_AT, M1_AT, XT_AT, LG_AT = ((5, 0), (6, 0)), (7, 0), (8, 0), (9, 0), (11, 0), (12, 0)
PROJ_AT = (Q_AT, QS_AT, K_AT, KS_AT)
M_AT = (M0_AT, M1_AT)
SUM_AT, HI_AT, LO_AT = ((1, 0), (2, 0)), ((3, 0), (3, 1)), ((4, 0), (4, 1))


def has(t, lag):
    return not isinstance(t, int) or 0 <= t + lag < NB


def later(t, lag):
    return not isinstance(t, int) or t + lag > 0


def maxima_of(t, s, k):
    lag, g = (1, 2 + s // 4) if s < 8 else (2, (s - 8) // 4)
    if not has(t, lag):
        return None
    jp, i = divmod(2 * (s % 4) + k, NC)
    return lag, g, jp, i, 8 * g + 4 * jp + i


def rstd(nc, dve, var, work):
    v, h, y = work[:, 0, :], work[:, 1, :], work[:, 2, :]
    nc.vector.tensor_scalar(v, var, EPS, None, ALU.add)
    dve.drain()
    nc.vector.tensor_scalar(h.bitcast(U32), v.bitcast(U32), 1, None, ALU.logical_shift_right)
    dve.drain()
    nc.vector.tensor_scalar(y.bitcast(I32), h.bitcast(I32), -1.0, float(0x5F3759DF), ALU.mult, ALU.add)
    dve.drain()
    for _ in range(3):
        nc.vector.tensor_tensor(h, y, y, ALU.mult)
        dve.drain()
        nc.vector.tensor_tensor(h, h, v, ALU.mult)
        dve.drain()
        nc.vector.tensor_scalar(h, h, -0.5, 1.5, ALU.mult, ALU.add)
        dve.drain()
        nc.vector.tensor_tensor(y, y, h, ALU.mult)
        dve.drain()
    return y


def moe_layer(nc, xT, xr, wqT, wqsT, wkT, wksT, wvT, woT, gwT, w1, w2, b1, b2, cosT, sinT, ident, selo, sele, out):
    ctx = ExitStack()
    with ctx:
        def sb(name, shape, dt=F32):
            return ctx.enter_context(nc.sbuf_tensor(name, shape, dt))

        def sem(name):
            return ctx.enter_context(nc.semaphore(name))

        wproj = sb("wproj", [P, 5, D])
        wo_sb = sb("wo_sb", [P, D])
        gw_sb = sb("gw_sb", [P, NE])
        cos_sb = sb("cos_sb", [P, S])
        sin_sb = sb("sin_sb", [P, S])
        id_sb = sb("id_sb", [P, P])
        selo_sb = sb("selo_sb", [P, 36])
        sele_f = sb("sele_f", [NE, NE * P])
        b1_sb = sb("b1_sb", [P, NX * NF])
        b2_sb = sb("b2_sb", [P, NX])
        x1 = sb("x1", [P, NCH, D])
        x1h = sb("x1h", [P, TOK], F32R)
        x1l = sb("x1l", [P, TOK], F32R)
        score = sb("score", [P, NCH, NE])
        loaded = sem("loaded")
        loads = ((wproj[:, 0, :], wqT), (wproj[:, 1, :], wqsT), (wproj[:, 2, :], wkT), (wproj[:, 3, :], wksT),
                 (wproj[:, 4, :], wvT), (wo_sb[:], woT), (gw_sb[:], gwT), (cos_sb[:], cosT), (sin_sb[:], sinT),
                 (id_sb[:], ident), (selo_sb[:], selo), (sele_f[:], sele), (b1_sb[:], b1), (b2_sb[:], b2))
        attention(nc, locals())
        experts(nc, locals())


def attention(nc, kept):
    (xT, xr, wproj, wo_sb, gw_sb, cos_sb, sin_sb, id_sb, selo_sb, x1, x1h, x1l, score, loaded, loads, out) = (
        kept[k] for k in ("xT", "xr", "wproj", "wo_sb", "gw_sb", "cos_sb", "sin_sb", "id_sb", "selo_sb", "x1", "x1h",
                          "x1l", "score", "loaded", "loads", "out"))
    ctx = ExitStack()
    with ctx:
        def sb(name, shape, dt=F32):
            return ctx.enter_context(nc.sbuf_tensor(name, shape, dt))

        def sem(name):
            return ctx.enter_context(nc.semaphore(name))

        idb = sb("idb", [P, P], BF16)
        maskb = sb("maskb", [P, P], BF16)
        xq = sb("xq", [P, S])
        xv = sb("xv", [P, S])
        xres = sb("xres", [P, NC, D])
        minus = sb("minus", [P, 1])
        rot = sb("rot", [P, 2, S])
        rsum = sb("rsum", [P, 2, S])
        den_hi = sb("den_hi", [P, 2, S], F32R)
        den_lo = sb("den_lo", [P, 2, S], F32R)
        qa = sb("qa", [P, NG, S], F32R)
        ka = sb("ka", [P, NG, S], F32R)
        qb = sb("qb", [P, NG, S], F32R)
        kb = sb("kb", [P, NG, S], F32R)
        vaug = sb("vaug", [P, NC, NH, 32])
        pexp = sb("pexp", [P, 2, 4, SEGW])
        oT = sb("oT", [P, NG, S])
        rmax = sb("rmax", [P, NC, NH])
        mT = [sb(f"mT{k}", [NH // 2, S]) for k in range(2)]
        m_hi = [sb(f"m_hi{k}", [NH // 2, S], F32R) for k in range(2)]
        m_lo = [sb(f"m_lo{k}", [NH // 2, S], F32R) for k in range(2)]
        rec = sb("rec", [P, 2, NH])
        attn = sb("attn", [P, NC, D])
        attnT = sb("attnT", [P, S])
        xn = sb("xn", [P, NC, D])
        res = sb("res", [P, NC, D])
        bst = sb("bst", [P, NC, 6])
        bag = sb("bag", [P, NC, 2])
        nw = sb("nw", [P, 4, NC])
        x1T = sb("x1T", [P, S])
        lg = sb("lg", [P, NC, NE])
        lsm = sb("lsm", [P, 2, NC])
        ps = ctx.enter_context(nc.psum_tensor("ps", [P, 8, 512], F32))
        MISC = 7

        ready = sem("ready")
        xq_in, xv_in, xr_in = sem("xq_in"), sem("xv_in"), sem("xr_in")
        proj_done = sem("proj_done")
        rope_mul = sem("rope_mul")
        rope_sum = sem("rope_sum")
        rope_hi = sem("rope_hi")
        rope_lo = sem("rope_lo")
        fill_a = [sem(f"fill_a{g}") for g in range(NG)]
        fill_b = [sem(f"fill_b{g}") for g in range(NG)]
        fill_m = [sem(f"fill_m{g}") for g in range(NG)]
        a_done = sem("a_done")
        a_max = sem("a_max")
        mt_done = sem("mt_done")
        mt_out = sem("mt_out")
        mhi_done = sem("mhi_done")
        mlo_done = sem("mlo_done")
        b_done = sem("b_done")
        b_exp = sem("b_exp")
        p_masked = sem("p_masked")
        pv_done = sem("pv_done")
        o_out = sem("o_out")
        v_done, v_out = sem("v_done"), sem("v_out")
        ot_done, ot_out = sem("ot_done"), sem("ot_out")
        at_done, at_out = sem("at_done"), sem("at_out")
        wo_done, r_done, n_done = sem("wo_done"), sem("r_done"), sem("n_done")
        xt_done, xt_out, x1_kept = sem("xt_done"), sem("xt_out"), sem("x1_kept")
        x1l_done = sem("x1l_done")
        lg_done, lg_sub, lg_exp, lg_fin = sem("lg_done"), sem("lg_sub"), sem("lg_exp"), sem("lg_fin")

        k_rows = sem("k_rows")
        sp_step, pool_step = sem("sp_step"), sem("pool_step")
        READY = 1
        block = ctx.enter_context(nc.Block())

        def bodies(eng, body):
            body(-2)
            body(-1)
            body(0)
            with eng.Fori(1, NB - 3) as t:
                body(t)
            body(NB - 3)
            body(NB - 2)
            body(NB - 1)
            body(NB)

        @block.sync
        def _(sp):
            for dst, src in loads:
                sp.dma_start(dst, src).then_inc(loaded, 16)

            def after(signal, value):
                sp.wait_ge(signal, value)
                sp.sem_inc(sp_step, 1)

            def body(t):
                for g in range(NG):
                    if has(t, 1):
                        if has(t, 0):
                            after(b_done, 48 * t + 12 * g + 12)
                        after(fill_a[g], 96 * (t + 2))
                        sp.dma_start(qb[:, g, :].bitcast(F32), qa[:, g, :].bitcast(F32)).then_inc(fill_b[g], 16)
                        sp.dma_start(kb[:, g, :].bitcast(F32), ka[:, g, :].bitcast(F32)).then_inc(fill_b[g], 16)
                        half, row = divmod(4 * g, NH // 2)
                        after(mlo_done, 2 * (t + 1) + half + 1)
                        after(fill_b[g], 32 * (t + 2))
                        sp.dma_start(qb[3:P:32, g, :].bitcast(F32), m_hi[half][row:row + 4, :].bitcast(F32)).then_inc(fill_m[g], 16)
                        sp.dma_start(qb[7:P:32, g, :].bitcast(F32), m_lo[half][row:row + 4, :].bitcast(F32)).then_inc(fill_m[g], 16)
                    if has(t, 2):
                        if has(t, 1):
                            after(a_done, 32 * (t + 1) + 8 * g + 8)
                        if g == 0:
                            after(rope_lo, 2 * (t + 3))
                            sp.wait_ge(k_rows, 1)
                        for which, stack in ((0, qa), (1, ka)):
                            parts = (den_hi, den_lo, den_hi) if which == 0 else (den_hi, den_hi, den_lo)
                            for r, part in enumerate(parts):
                                sp.dma_start(stack[r:P:4, g, :].bitcast(F32),
                                             part[32 * g:32 * g + 32, which, :].bitcast(F32)).then_inc(fill_a[g], 16)
                    if g == 0 and has(t, 3):
                        if later(t, 3):
                            after(proj_done, 4 * (t + 3))
                        sp.dma_start(xq[:], xT[:, bass.ds((t + 3) * S, S)]).then_inc(xq_in, 16)
                    if g == 1 and has(t, 1):
                        if later(t, 1):
                            after(v_done, t + 1)
                        sp.dma_start(xv[:], xT[:, bass.ds((t + 1) * S, S)]).then_inc(xv_in, 16)
                    if g == 3 and has(t, 0):
                        if later(t, 0):
                            after(r_done, t)
                        sp.dma_start(xres[:], xr[bass.ds(t * S, S), :].rearrange("(c p) d -> p c d", p=P)).then_inc(xr_in, 16)
                if has(t, -1):
                    after(n_done, t)
                    sp.dma_start(x1[:, bass.ds((t - 1) * NC, NC), :], xn[:]).then_inc(x1_kept, 16)

            sp.dma_start(xq[:], xT[:, 0:S]).then_inc(xq_in, 16)
            bodies(nc.sync, body)

        @block.gpsimd
        def _(pool):
            nc.gpsimd.memset(idb[:], 0.0)
            nc.gpsimd.memset(maskb[:], 0.0)
            nc.gpsimd.memset(vaug[:], 0.0)
            nc.gpsimd.memset(qa[:].bitcast(F32), 0.0)
            pool.drain()
            nc.gpsimd.affine_select(out=idb[:], in_=idb[:], compare_op=ALU.not_equal, fill=1.0, base=0,
                                    pattern=[[-1, P]], channel_multiplier=1)
            nc.gpsimd.affine_select(out=maskb[:], in_=maskb[:], compare_op=ALU.is_ge, fill=NEG, base=0,
                                    pattern=[[-1, P]], channel_multiplier=1)
            nc.gpsimd.memset(vaug[:, :, :, 8:9], 1.0)
            nc.gpsimd.memset(minus[:], 0.0)
            for row in [32 * j + r for j in range(4) for r in (3, 7)]:
                pool.drain()
                nc.gpsimd.affine_select(out=minus[:], in_=minus[:], compare_op=ALU.not_equal, fill=-1.0, base=-row,
                                        pattern=[[0, 1]], channel_multiplier=1)
            pool.drain()
            nc.gpsimd.affine_select(out=maskb[:], in_=maskb[:], compare_op=ALU.is_ge, fill=NEG, base=0,
                                    pattern=[[-1, P]], channel_multiplier=1).then_inc(ready, 1)

            def place(t, at):
                s, k = at
                g, u = divmod(s, 4)
                if has(t, 0) and u == 0 and k == 0 and g > 0:
                    mask(t, g - 1)
                if has(t, 0) and at == (15, 1):
                    mask(t, NG - 1)
                if has(t, 2) and at in SUM_AT:
                    n, w = t + 2, SUM_AT.index(at)
                    pool.wait_ge(rope_mul, 4 * n + 2 * w + 2)
                    nc.gpsimd.tensor_tensor(rsum[:, w, :], rot[:, 0, :], rot[:, 1, :], ALU.add).then_inc(rope_sum, 1)
                if has(t, 2) and at in LO_AT:
                    n, w = t + 2, LO_AT.index(at)
                    pool.wait_ge(rope_hi, 2 * n + w + 1)
                    nc.gpsimd.tensor_tensor(den_lo[:, w, :], rsum[:, w, :], den_hi[:, w, :].bitcast(F32),
                                            ALU.subtract).then_inc(rope_lo, 1)
                if has(t, -1) and at == (XT_AT[0] + 1, 0):
                    pool.wait_ge(xt_out, 2 * t)
                    nc.gpsimd.tensor_tensor(x1l[:, bass.ds((t - 1) * S, S)], x1T[:],
                                            x1h[:, bass.ds((t - 1) * S, S)].bitcast(F32), ALU.subtract).then_inc(x1l_done, 1)
                if has(t, 1) and (s - 1, k) in M_AT:
                    half = M_AT.index((s - 1, k))
                    pool.wait_ge(mt_out, 4 * (t + 1) + 2 * half + 2)
                    nc.gpsimd.tensor_tensor(m_lo[half][:], mT[half][:], m_hi[half][:].bitcast(F32), ALU.subtract).then_inc(mlo_done, 1)

            def mask(t, g):
                pool.wait_ge(b_exp, 48 * t + 12 * g + 12)
                pool.sem_inc(pool_step, 1)
                for i in range(NC):
                    blk = pexp[:, g % 2, :, SEG[i]:SEG[i] + P]
                    nc.gpsimd.affine_select(out=blk, in_=blk, compare_op=ALU.is_ge, fill=0.0, base=0,
                                            pattern=[[0, 4], [1, P]], channel_multiplier=-1).then_inc(p_masked, 1)

            def body(t):
                for s in range(16):
                    for k in range(2):
                        place(t, (s, k))

            bodies(nc.gpsimd, body)

        @block.scalar
        def _(act):
            def exponentials(t, s, k):
                g, u = divmod(s, 4)
                act.wait_ge(b_done, 48 * t + 3 * s + k + 1)
                if k == 0 and u == 0 and (g > 1 or later(t, 0)):
                    act.wait_ge(pv_done, 4 * t + g - 1)
                blocks = BSTEPS[k]
                first, width = SEG[blocks[0]], sum(S - P * i for i in blocks)
                nc.scalar.activation(pexp[:, g % 2, u, first:first + width], ps[:, 4 + (3 * s + k) % 2, 0:width],
                                     ACT.Exp, scale=SCALE).then_inc(b_exp, 1)

            def place(t, at):
                if has(t, 2) and at in HI_AT:
                    n, w = t + 2, HI_AT.index(at)
                    act.wait_ge(rope_sum, 2 * n + w + 1)
                    if w == 0 and later(t, 2):
                        for g in range(NG):
                            act.wait_ge(fill_a[g], 96 * n)
                    nc.scalar.activation(den_hi[:, w, :], rsum[:, w, :], ACT.Copy).then_inc(rope_hi, 1)
                if has(t, 0) and at == V_AT:
                    act.wait_ge(v_done, t + 1)
                    if later(t, 0):
                        act.wait_ge(pv_done, 4 * t)
                    else:
                        act.wait_ge(ready, READY)
                    nc.scalar.activation(vaug[:, :, :, 0:DK], ps[:, MISC, :].rearrange("p (c h d) -> p c h d", c=NC, d=DK),
                                         ACT.Copy).then_inc(v_out, 1)
                if has(t, -1) and at == AT_AT:
                    act.wait_ge(at_done, t)
                    nc.scalar.activation(attnT[:], ps[:, MISC, :], ACT.Copy).then_inc(at_out, 1)
                if has(t, -1) and at == XT_AT:
                    act.wait_ge(xt_done, t)
                    if later(t, -1):
                        act.wait_ge(x1l_done, t - 1)
                    nc.scalar.activation(x1T[:], ps[:, MISC, :], ACT.Copy).then_inc(xt_out, 1)
                    nc.scalar.activation(x1h[:, bass.ds((t - 1) * S, S)], ps[:, MISC, :], ACT.Copy).then_inc(xt_out, 1)
                if has(t, -1) and at == LG_AT:
                    act.wait_ge(lg_sub, t)
                    nc.scalar.activation(lg[:], lg[:], ACT.Exp).then_inc(lg_exp, 1)
                if has(t, 1) and at in M_AT:
                    half = M_AT.index(at)
                    act.wait_ge(mt_done, 2 * (t + 1) + half + 1)
                    if later(t, 1):
                        for g in (2 * half, 2 * half + 1):
                            act.wait_ge(fill_m[g], 32 * (t + 1))
                    nc.scalar.activation(mT[half][:], ps[0:NH // 2, MISC, :], ACT.Copy).then_inc(mt_out, 1)
                    nc.scalar.activation(m_hi[half][:], ps[0:NH // 2, MISC, :], ACT.Copy).then_inc(mt_out, 1)

            def body(t):
                for s in range(16):
                    g, u = divmod(s, 4)
                    if u == 0 and g > 1 and has(t, 0):
                        act.wait_ge(pv_done, 4 * t + g - 1)
                        if g == 2 and later(t, 0):
                            act.wait_ge(ot_done, 2 * t)
                        nc.scalar.activation(oT[:, g - 2, :], ps[:, 6, :], ACT.Copy).then_inc(o_out, 1)
                    if u == 0 and g < 2 and has(t, -1):
                        act.wait_ge(pv_done, 4 * t + g - 1)
                        nc.scalar.activation(oT[:, 2 + g, :], ps[:, 6, :], ACT.Copy).then_inc(o_out, 1)
                    for k in range(3):
                        if has(t, 0):
                            exponentials(t, s, k)
                        if k < 2:
                            place(t, (s, k))

            bodies(nc.scalar, body)

        @block.tensor
        def _(pe):
            pe.wait_ge(loaded, 16 * len(loads))
            pe.wait_ge(ready, READY)

            def maxima(t, s, k):
                if (step := maxima_of(t, s, k)) is None:
                    return
                lag, g, jp, i, number = step
                if i == 0 and jp == 0:
                    pe.wait_ge(fill_a[g], 96 * (t + lag + 1))
                if later(t, lag) or number >= 2:
                    pe.wait_ge(a_max, 32 * (t + lag) + number - 1)
                bank = 2 * (number % 2)
                for j in range(2):
                    row = 32 * (2 * jp + j)
                    nc.tensor.matmul(ps[:, bank + j, 0:P * (i + 1)], qa[row:row + 32, g, P * i:P * (i + 1)],
                                     ka[row:row + 32, g, 0:P * (i + 1)], start=True, stop=False)
                for j in range(2):
                    last = nc.tensor.matmul(ps[:, bank + j, P * i:P * (i + 1)], idb[:], maskb[:], start=False, stop=True)
                last.then_inc(a_done, 1)

            def exponents(t, s, k):
                g, u = divmod(s, 4)
                if u == 0 and k == 0:
                    pe.wait_ge(fill_b[g], 32 * (t + 1))
                    pe.wait_ge(fill_m[g], 32 * (t + 1))
                row, step = 32 * u, 3 * s + k
                if later(t, 0) or step >= 2:
                    pe.wait_ge(b_exp, 48 * t + step - 1)
                at = 0
                for i in BSTEPS[k]:
                    last = nc.tensor.matmul(ps[:, 4 + step % 2, at:at + S - P * i], kb[row:row + 32, g, P * i:P * (i + 1)],
                                            qb[row:row + 32, g, P * i:S], start=(at == 0), stop=True, skip_group_check=True)
                    at += S - P * i
                last.then_inc(b_done, 1)

            def values(t, g, i):
                if i == 0:
                    pe.wait_ge(p_masked, 16 * t + 4 * g + 4)
                    if g > 0 or later(t, 0):
                        pe.wait_ge(o_out, 4 * t + g)
                    if g == 0:
                        pe.wait_ge(v_out, t + 1)
                for j in range(4):
                    last = nc.tensor.matmul(ps[32 * j:32 * j + 32, 6, P * i:S], vaug[:, i, 4 * g + j, :],
                                            pexp[:, g % 2, j, SEG[i]:SEG[i] + S - P * i], start=(i == 0), stop=(i == NC - 1),
                                            skip_group_check=True)
                if i == NC - 1:
                    last.then_inc(pv_done, 1)

            def place(t, at):
                if has(t, 2) and at in PROJ_AT:
                    n, w = t + 2, PROJ_AT.index(at)
                    if w == 0:
                        pe.wait_ge(xq_in, 16 * (n + 1))
                        if has(t, -2):
                            pe.wait_ge(lg_sub, t - 1)
                        elif has(t, 0):
                            pe.wait_ge(mt_out, 4 * (t + 1))
                        elif later(t, 2):
                            pe.wait_ge(rope_mul, 4 * n)
                    else:
                        pe.wait_ge(rope_mul, 4 * n + w)
                    nc.tensor.matmul(ps[:, MISC, :], wproj[:, w, :], xq[:], start=True, stop=True).then_inc(proj_done, 1)
                if has(t, 1) and at in M_AT:
                    half = M_AT.index(at)
                    pe.wait_ge(a_max, 32 * (t + 1) + 16 * (half + 1))
                    if half == 0:
                        if has(t, 2):
                            pe.wait_ge(rope_mul, 4 * (t + 3))
                        else:
                            pe.wait_ge(lg_sub, t - 1)
                    elif has(t, -1):
                        pe.wait_ge(r_done, t)
                    elif has(t, 0):
                        pe.wait_ge(v_out, t + 1)
                    else:
                        pe.wait_ge(mt_out, 4 * (t + 1) + 2)
                    for c in range(NC):
                        last = nc.tensor.transpose(ps[0:NH // 2, MISC, P * c:P * (c + 1)],
                                                   rmax[:, c, 8 * half:8 * half + 8], id_sb[:])
                    last.then_inc(mt_done, 1)
                if has(t, 0) and at == V_AT:
                    if has(t, 1):
                        pe.wait_ge(mt_out, 4 * (t + 1) + 2)
                    else:
                        pe.wait_ge(lg_sub, t - 1)
                    pe.wait_ge(xv_in, 16 * (t + 1))
                    for c in range(NC):
                        last = nc.tensor.matmul(ps[:, MISC, P * c:P * (c + 1)], xv[:, P * c:P * (c + 1)], wproj[:, 4, :],
                                                start=True, stop=True)
                    last.then_inc(v_done, 1)
                if has(t, -1) and at in OT_AT:
                    half = OT_AT.index(at)
                    if half == 0:
                        pe.wait_ge(o_out, 4 * t)
                        if has(t, 0):
                            pe.wait_ge(v_out, t + 1)
                        else:
                            pe.wait_ge(lg_sub, t - 1)
                    else:
                        pe.wait_ge(ot_out, 2 * (t - 1) + 1)
                    for c in range(2):
                        for g in range(NG):
                            to = (c * NG + g) * 36
                            last = nc.tensor.matmul(ps[:, MISC, to:to + 36], oT[:, g, P * (2 * half + c):P * (2 * half + c + 1)],
                                                    selo_sb[:], start=True, stop=True)
                    last.then_inc(ot_done, 1)
                if has(t, -1) and at == AT_AT:
                    pe.wait_ge(ot_out, 2 * t)
                    for c in range(NC):
                        last = nc.tensor.transpose(ps[:, MISC, P * c:P * (c + 1)], attn[:, c, :], id_sb[:])
                    last.then_inc(at_done, 1)
                if has(t, -1) and at == WO_AT:
                    pe.wait_ge(at_out, t)
                    for c in range(NC):
                        last = nc.tensor.matmul(ps[:, MISC, P * c:P * (c + 1)], attnT[:, P * c:P * (c + 1)], wo_sb[:],
                                                start=True, stop=True)
                    last.then_inc(wo_done, 1)
                if has(t, -1) and at == XT_AT:
                    pe.wait_ge(n_done, t)
                    if has(t, 1):
                        pe.wait_ge(mt_out, 4 * (t + 2))
                    for c in range(NC):
                        last = nc.tensor.transpose(ps[:, MISC, P * c:P * (c + 1)], xn[:, c, :], id_sb[:])
                    last.then_inc(xt_done, 1)
                if has(t, -1) and at == LG_AT:
                    pe.wait_ge(xt_out, 2 * t)
                    for c in range(NC):
                        last = nc.tensor.matmul(ps[:, MISC, NE * c:NE * (c + 1)], x1T[:, P * c:P * (c + 1)], gw_sb[:],
                                                start=True, stop=True)
                    last.then_inc(lg_done, 1)

            def body(t):
                for s in range(16):
                    g, u = divmod(s, 4)
                    for k in range(3):
                        if has(t, 0):
                            exponents(t, s, k)
                        if k < 2:
                            maxima(t, s, k)
                            place(t, (s, k))
                    if g > 0 and has(t, 0):
                        values(t, g - 1, u)
                    if g == 0 and has(t, -1):
                        values(t - 1, NG - 1, u)

            bodies(nc.tensor, body)

        @block.vector
        def _(dve):
            dve.wait_ge(ready, READY)
            nc.vector.tensor_copy(ka[:].rearrange("p g n -> p (g n)"), minus[:].to_broadcast([P, NG * S])).then_inc(k_rows, 1)
            dve.wait_ge(loaded, 16 * len(loads))

            def maxima(t, s, k):
                if (step := maxima_of(t, s, k)) is None:
                    return
                lag, g, jp, i, number = step
                dve.wait_ge(a_done, 32 * (t + lag) + number + 1)
                if number % 16 == 0 and later(t, lag):
                    dve.wait_ge(mt_done, 2 * (t + lag - 1) + number // 16 + 1)
                bank = 2 * (number % 2)
                nc.vector.tensor_reduce(rmax[:, i, 4 * g + 2 * jp:4 * g + 2 * jp + 2],
                                        ps[:, bank:bank + 2, 0:P * (i + 1)], AX.X, ALU.max).then_inc(a_max, 1)

            def place(t, at):
                if has(t, 2) and at in PROJ_AT:
                    n, w = t + 2, PROJ_AT.index(at)
                    dve.wait_ge(proj_done, 4 * n + w + 1)
                    if w % 2 == 0 and (w == 2 or later(t, 2)):
                        dve.wait_ge(rope_sum, 2 * n + w // 2)
                    nc.vector.tensor_tensor(rot[:, w % 2, :], ps[:, MISC, :], (cos_sb if w % 2 == 0 else sin_sb)[:],
                                            ALU.mult).then_inc(rope_mul, 1)
                if has(t, -1) and at in OT_AT:
                    half = OT_AT.index(at)
                    dve.wait_ge(ot_done, 2 * (t - 1) + half + 1)
                    if half == 0 and later(t, -1):
                        dve.wait_ge(at_done, t - 1)
                    sums = ps[:, MISC, 0:8 * 36].rearrange("p (c h k) -> p c h k", c=2, k=9)
                    nc.vector.reciprocal(rec[:], sums[:, :, :, 8])
                    dve.drain()
                    nc.vector.tensor_tensor(attn[:, 2 * half:2 * half + 2, :].rearrange("p c (h d) -> p c h d", d=DK),
                                            sums[:, :, :, 0:DK], rec[:].unsqueeze(3).to_broadcast([P, 2, NH, DK]),
                                            ALU.mult).then_inc(ot_out, 1)
                    dve.drain()
                if has(t, -1) and at == WO_AT:
                    dve.wait_ge(wo_done, t)
                    dve.wait_ge(xr_in, 16 * t)
                    nc.vector.tensor_tensor(res[:].rearrange("p c d -> p (c d)"), ps[:, MISC, :],
                                            xres[:].rearrange("p c d -> p (c d)"), ALU.add).then_inc(r_done, 1)
                    dve.drain()
                    for c in range(NC):
                        nc.vector.bn_stats(bst[:, c, :], res[:, c, :])
                    dve.drain()
                    for c in range(NC):
                        nc.vector.bn_aggr(bag[:, c, :], bst[:, c, :])
                    dve.drain()
                    y = rstd(nc, dve, bag[:, :, 1], nw)
                    if later(t, -1):
                        dve.wait_ge(xt_done, t - 1)
                        dve.wait_ge(x1_kept, 16 * (t - 1))
                    for c in range(NC):
                        last = nc.vector.tensor_scalar(xn[:, c, :], res[:, c, :], bag[:, c, 0:1], y[:, c:c + 1],
                                                       ALU.subtract, ALU.mult)
                    last.then_inc(n_done, 1)
                if has(t, -1) and at == LG_AT:
                    dve.wait_ge(lg_done, t)
                    logits = ps[:, MISC, 0:NC * NE].rearrange("p (c e) -> p c e", e=NE)
                    nc.vector.tensor_reduce(lsm[:, 0, :], logits, AX.X, ALU.max)
                    dve.drain()
                    nc.vector.tensor_tensor(lg[:], logits, lsm[:, 0, :].unsqueeze(2).to_broadcast([P, NC, NE]),
                                            ALU.subtract).then_inc(lg_sub, 1)
                    dve.wait_ge(lg_exp, t)
                    nc.vector.tensor_reduce(lsm[:, 1, :], lg[:], AX.X, ALU.add)
                    dve.drain()
                    nc.vector.reciprocal(lsm[:, 0, :], lsm[:, 1, :])
                    dve.drain()
                    dst = score[:, bass.ds((t - 1) * NC, NC), :]
                    nc.vector.tensor_tensor(dst, lg[:], lsm[:, 0, :].unsqueeze(2).to_broadcast([P, NC, NE]),
                                            ALU.mult).then_inc(lg_fin, 1)
                    dve.drain()

            def body(t):
                for s in range(16):
                    for k in range(2):
                        maxima(t, s, k)
                        place(t, (s, k))

            bodies(nc.vector, body)


def experts(nc, kept):
    (w1, w2, sele_f, id_sb, b1_sb, b2_sb, x1, x1h, x1l, score, out) = (
        kept[k] for k in ("w1", "w2", "sele_f", "id_sb", "b1_sb", "b2_sb", "x1", "x1h", "x1l", "score", "out"))
    NT = TOK // S
    BITS = 30
    NS = NCH * NE
    ctx = ExitStack()
    with ctx:
        def sb(name, shape, dt=F32):
            return ctx.enter_context(nc.sbuf_tensor(name, shape, dt))

        def sem(name):
            return ctx.enter_context(nc.semaphore(name))

        ones = sb("ones", [P, P])
        before = sb("before", [P, P])
        ones_row = sb("ones_row", [P, NS])
        thr, trial, cand, need = (sb(n, [P, 1]) for n in ("thr", "trial", "cand", "need"))
        count = sb("count", [P, 1])
        hit = sb("hit", [P, NS])
        equal = sb("equal", [P, NE, NCH])
        rank = sb("rank", [P, NS])
        upto = sb("upto", [P, NS])
        gate = sb("gate", [P, NCH, NE])
        gT_hi = sb("gT_hi", [NE, TOK], F32R)
        gT_lo = sb("gT_lo", [NE, TOK], F32R)
        w_stage = sb("w_stage", [P, 2, F])
        b1_cur = sb("b1_cur", [P, 2, NF])
        sel_cur = sb("sel_cur", [NE, 2, P], F32R)
        w1h, w1l, w2h, w2l = (sb(n, [P, 2, F], F32R) for n in ("w1h", "w1l", "w2h", "w2l"))
        acc = sb("acc", [P, TOK])
        h = sb("h", [P, NF, S])
        hh = sb("hh", [P, 2, NF, S], F32R)
        hl = sb("hl", [P, 2, NF, S], F32R)
        gbc = sb("gbc", [P, 2, S])
        part = sb("part", [P, 2, S])
        res2 = sb("res2", [P, NCH, D])
        bst2 = sb("bst2", [P, NCH, 6])
        bag2 = sb("bag2", [P, NCH, 2])
        nw2 = sb("nw2", [P, 3, NCH])
        pe_ps = ctx.enter_context(nc.psum_tensor("pe_ps", [P, 8, 512], F32))

        built = sem("built")
        counted, totalled = sem("counted"), sem("totalled")
        eq_done, eq_sums, gate_done = sem("eq_done"), sem("eq_sums"), sem("gate_done")
        gt_tr, gt_hi, gt_lo = sem("gt_tr"), sem("gt_hi"), sem("gt_lo")
        w_in, w_split = sem("w_in"), sem("w_split")
        up_done, gelu_done = sem("up_done"), sem("gelu_done")
        hh_done, hl_done = sem("hh_done"), sem("hl_done")
        down_done, y_done = sem("down_done"), sem("y_done")
        g_done, g_out, acc_done = sem("g_done"), sem("g_out"), sem("acc_done")
        fin_tr, fin_in, fin_ready, stored = sem("fin_tr"), sem("fin_in"), sem("fin_ready"), sem("stored")
        sp_turn = sem("sp_turn")
        block = ctx.enter_context(nc.Block())

        def after(eng, signal, value):
            if not isinstance(value, int) or value > 0:
                eng.wait_ge(signal, value)

        def all_experts(eng, expert):
            expert(0, 0)
            expert(1, 1)
            with eng.Fori(0, (NE - 2) // 2) as i:
                expert(2 * i + 2, 0)
                expert(2 * i + 3, 1)
            expert(NE, 0)

        @block.sync
        def _(sp):
            def load(e):
                sp.dma_start(w_stage[:, 0, :], w1[:, bass.ds(e * F, F)]).then_inc(w_in, 16)
                sp.dma_start(w_stage[:, 1, :], w2[:, bass.ds(e * F, F)]).then_inc(w_in, 16)

            load(0)

            def expert(e, buf):
                if isinstance(e, int) and e == NE:
                    return
                sp.wait_ge(w_split, e + 1)
                sp.sem_inc(sp_turn, 1)
                load(e + 1)

            all_experts(nc.sync, expert)
            for c in range(8):
                sp.wait_ge(fin_ready, c + 1)
                sp.dma_start(out[c * S:(c + 1) * S, :].rearrange("(c p) d -> p c d", p=P), res2[:, NC * c:NC * c + NC, :])\
                  .then_inc(stored, 16)
            sp.wait_ge(stored, 16 * 8)

        @block.gpsimd
        def _(pool):
            nc.gpsimd.memset(ones[:], 1.0)
            nc.gpsimd.memset(ones_row[:], 1.0)
            nc.gpsimd.memset(before[:], 1.0)
            pool.drain()
            nc.gpsimd.affine_select(out=before[:], in_=before[:], compare_op=ALU.is_gt, fill=0.0, base=0,
                                    pattern=[[1, P]], channel_multiplier=-1).then_inc(built, 1)

            def expert(e, buf):
                if isinstance(e, int) and e == 0:
                    return
                for t in range(NT):
                    u = NT * e + t
                    pool.wait_ge(y_done, u + 1)
                    nc.gpsimd.tensor_tensor(acc[:, t * S:(t + 1) * S], acc[:, t * S:(t + 1) * S], part[:, t % 2, :],
                                            ALU.add).then_inc(acc_done, 1)

            all_experts(nc.gpsimd, expert)

        @block.scalar
        def _(act):
            for k in range(NT):
                act.wait_ge(gt_tr, k + 1)
                nc.scalar.activation(gT_hi[:, k * S:(k + 1) * S], pe_ps[0:NE, k, :], ACT.Copy).then_inc(gt_hi, 1)

            def expert(e, buf):
                for t in range(NT):
                    u = NT * e + t
                    for f in range(NF):
                        act.wait_ge(up_done, NF * u + f + 1)
                        after(act, hl_done, NF * (u - 1) + f + 1)
                        nc.scalar.activation(h[:, f, :], pe_ps[:, f, :], ACT.Gelu_apprx_tanh,
                                             bias=b1_cur[:, buf, f:f + 1]).then_inc(gelu_done, 1)
                    if not isinstance(e, int) or e > 0:
                        act.wait_ge(g_done, u - NT + 1)
                        act.wait_ge(y_done, u - 1)
                        nc.scalar.activation(gbc[:, t % 2, :], pe_ps[:, 6, :], ACT.Copy).then_inc(g_out, 1)

            all_experts(nc.scalar, expert)

        @block.tensor
        def _(pe):
            pe.wait_ge(built, 1)
            for k in range(BITS + 1):
                pe.wait_ge(counted, k + 1)
                nc.tensor.matmul(pe_ps[:, 7, 0:1], ones[:], count[:], start=True, stop=True).then_inc(totalled, 1)
            pe.wait_ge(eq_done, 1)
            nc.tensor.matmul(pe_ps[:, 5, 0:NS], ones[:], equal[:].rearrange("p e c -> p (e c)"), start=True, stop=True)
            nc.tensor.matmul(pe_ps[:, 6, 0:NS], before[:], equal[:].rearrange("p e c -> p (e c)"),
                             start=True, stop=True).then_inc(eq_sums, 1)
            pe.wait_ge(gate_done, 1)
            for k in range(NT):
                for c in range(NC):
                    last = nc.tensor.transpose(pe_ps[0:NE, k, P * c:P * (c + 1)], gate[:, NC * k + c, :], id_sb[:])
                last.then_inc(gt_tr, 1)
            pe.wait_ge(gt_lo, NT)

            def down(e, buf, t):
                u = NT * e + t
                after(pe, y_done, u - 1)
                n = 0
                for f in range(NF):
                    w = slice(P * f, P * (f + 1))
                    pe.wait_ge(hl_done, NF * u + f + 1)
                    for a, b in ((w2h, hh), (w2l, hh), (w2h, hl)):
                        last = nc.tensor.matmul(pe_ps[:, 4 + t % 2, :], a[:, buf, w], b[:, t % 2, f, :],
                                                start=(n == 0), stop=(n == 3 * NF - 1))
                        n += 1
                last.then_inc(down_done, 1)

            def final(t):
                pe.wait_ge(acc_done, NT * (NE - 1) + t + 1)
                after(pe, fin_in, t)
                for c in range(NC):
                    last = nc.tensor.transpose(pe_ps[:, 7, P * c:P * (c + 1)], acc[:, t * S + P * c:t * S + P * (c + 1)], id_sb[:])
                last.then_inc(fin_tr, 1)

            def expert(e, buf):
                pe.wait_ge(w_split, e + 1)
                for t in range(NT):
                    u = NT * e + t
                    for f in range(NF):
                        w = slice(P * f, P * (f + 1))
                        after(pe, gelu_done, NF * (u - 1) + f + 1)
                        xs = slice(t * S, (t + 1) * S)
                        for n, (a, b) in enumerate(((w1h, x1h), (w1l, x1h), (w1h, x1l))):
                            last = nc.tensor.matmul(pe_ps[:, f, :], a[:, buf, w], b[:, xs], start=(n == 0), stop=(n == 2))
                        last.then_inc(up_done, 1)
                    if not isinstance(e, int) or e > 0:
                        if not isinstance(e, int) or u > NT:
                            pe.wait_ge(g_out, u - NT)
                        nc.tensor.matmul(pe_ps[:, 6, :], sel_cur[:, buf, :], gT_hi[:, xs], start=True, stop=False)
                        nc.tensor.matmul(pe_ps[:, 6, :], sel_cur[:, buf, :], gT_lo[:, xs], start=False, stop=True)\
                          .then_inc(g_done, 1)
                    if t > 0:
                        down(e, buf, t - 1)
                    elif not isinstance(e, int) or e > 0:
                        down(e - 1, 1 - buf, NT - 1)
                    if isinstance(e, int) and e == NE and t >= 3:
                        final(t - 3)

            all_experts(nc.tensor, expert)
            down(NE, 0, NT - 1)
            for t in range(NT - 3, NT):
                final(t)

        @block.vector
        def _(dve):
            def split(e, buf):
                dve.wait_ge(w_in, 32 * (e + 1))
                for w, hi in ((0, w1h), (1, w2h)):
                    nc.vector.tensor_copy(hi[:, buf, :], w_stage[:, w, :])
                nc.vector.tensor_copy(b1_cur[:, buf, :], b1_sb[:, bass.ds(e * NF, NF)])
                if not isinstance(e, int) or e > 0:
                    nc.vector.tensor_copy(sel_cur[:, buf, :], sele_f[:, bass.ds((e - 1) * P, P)])
                dve.drain()
                for w, hi, lo in ((0, w1h, w1l), (1, w2h, w2l)):
                    last = nc.vector.tensor_tensor(lo[:, buf, :], w_stage[:, w, :], hi[:, buf, :].bitcast(F32), ALU.subtract)
                last.then_inc(w_split, 1)

            split(0, 0)
            dve.wait_ge(built, 1)
            flat = score[:].rearrange("p c e -> p (c e)")
            nc.vector.memset(thr[:].bitcast(U32), 0)
            dve.drain()
            for k in range(BITS):
                nc.vector.tensor_scalar(trial[:].bitcast(U32), thr[:].bitcast(U32), 1 << (BITS - 1 - k), None, ALU.bitwise_or)
                dve.drain()
                nc.vector.tensor_scalar(hit[:], flat, trial[:, 0:1], 0.0, ALU.is_ge, ALU.add, accum_out=count[:])\
                  .then_inc(counted, 1)
                dve.wait_ge(totalled, k + 1)
                nc.vector.scalar_tensor_tensor(cand[:], pe_ps[:, 7, 0:1], float(TOPK), trial[:], ALU.is_ge, ALU.mult)
                dve.drain()
                nc.vector.tensor_tensor(thr[:], thr[:], cand[:], ALU.max)
                dve.drain()
            nc.vector.tensor_scalar(hit[:], flat, thr[:, 0:1], 0.0, ALU.is_gt, ALU.add, accum_out=count[:]).then_inc(counted, 1)
            nc.vector.tensor_scalar(equal[:].rearrange("p e c -> p c e"), score[:], thr[:, 0:1], None, ALU.is_equal)\
              .then_inc(eq_done, 1)
            dve.wait_ge(totalled, BITS + 1)
            nc.vector.tensor_scalar(need[:], pe_ps[:, 7, 0:1], -1.0, float(TOPK), ALU.mult, ALU.add)
            dve.wait_ge(eq_sums, 1)
            nc.vector.tensor_tensor_scan(upto[:], ones_row[:], pe_ps[:, 5, 0:NS], 0.0, ALU.mult, ALU.add)
            dve.drain()
            nc.vector.tensor_tensor(upto[:], upto[:], pe_ps[:, 5, 0:NS], ALU.subtract)
            dve.drain()
            nc.vector.tensor_tensor(rank[:], upto[:], pe_ps[:, 6, 0:NS], ALU.add)
            dve.drain()
            nc.vector.scalar_tensor_tensor(upto[:], rank[:], need[:, 0:1], equal[:].rearrange("p e c -> p (e c)"),
                                           ALU.is_lt, ALU.mult)
            dve.drain()
            nc.vector.tensor_tensor(gate[:], hit[:].rearrange("p (c e) -> p c e", e=NE),
                                    upto[:].rearrange("p (e c) -> p c e", e=NE), ALU.add)
            dve.drain()
            nc.vector.tensor_tensor(gate[:], gate[:], score[:], ALU.mult).then_inc(gate_done, 1)
            for k in range(NT):
                dve.wait_ge(gt_hi, k + 1)
                nc.vector.tensor_tensor(gT_lo[:, k * S:(k + 1) * S], pe_ps[0:NE, k, :], gT_hi[:, k * S:(k + 1) * S].bitcast(F32),
                                        ALU.subtract).then_inc(gt_lo, 1)

            def gated(e, t):
                u = NT * e + t
                dve.wait_ge(down_done, u + 1)
                if isinstance(e, int) and e == 0:
                    nc.vector.tensor_scalar(acc[:, t * S:(t + 1) * S], pe_ps[:, 4 + t % 2, :], b2_sb[:, 0:1], None, ALU.add)\
                      .then_inc(y_done, 1)
                    return
                dve.wait_ge(g_out, u - NT + 1)
                after(dve, acc_done, u - NT - 1)
                nc.vector.scalar_tensor_tensor(part[:, t % 2, :], pe_ps[:, 4 + t % 2, :], b2_sb[:, bass.ds(e, 1)],
                                               gbc[:, t % 2, :], ALU.add, ALU.mult).then_inc(y_done, 1)

            def final(t):
                dve.wait_ge(fin_tr, t + 1)
                rows = res2[:, NC * t:NC * (t + 1), :].rearrange("p c d -> p (c d)")
                nc.vector.tensor_tensor(rows, pe_ps[:, 7, :], x1[:, NC * t:NC * (t + 1), :].rearrange("p c d -> p (c d)"),
                                        ALU.add).then_inc(fin_in, 1)
                dve.drain()
                for c in range(NC * t, NC * (t + 1)):
                    nc.vector.bn_stats(bst2[:, c, :], res2[:, c, :])
                dve.drain()
                for c in range(NC * t, NC * (t + 1)):
                    nc.vector.bn_aggr(bag2[:, c, :], bst2[:, c, :])

            def expert(e, buf):
                for t in range(NT):
                    u = NT * e + t
                    after(dve, down_done, u - 1)
                    for f in range(NF + 1):
                        if f < NF:
                            dve.wait_ge(gelu_done, NF * u + f + 1)
                            nc.vector.tensor_copy(hh[:, t % 2, f, :], h[:, f, :]).then_inc(hh_done, 1)
                        if f > 0:
                            dve.wait_ge(hh_done, NF * u + f)
                            nc.vector.tensor_tensor(hl[:, t % 2, f - 1, :], h[:, f - 1, :],
                                                    hh[:, t % 2, f - 1, :].bitcast(F32), ALU.subtract).then_inc(hl_done, 1)
                    if t > 0:
                        gated(e, t - 1)
                    elif not isinstance(e, int) or e > 0:
                        gated(e - 1, NT - 1)
                    if t == 3 and (not isinstance(e, int) or e < NE):
                        split(e + 1, 1 - buf)
                    if isinstance(e, int) and e == NE and t >= 3:
                        final(t - 3)

            all_experts(nc.vector, expert)
            gated(NE, NT - 1)
            for t in range(NT - 3, NT):
                final(t)
            dve.drain()
            y = rstd(nc, dve, bag2[:, :, 1], nw2)
            for c in range(NCH):
                last = nc.vector.tensor_scalar(res2[:, c, :], res2[:, c, :], bag2[:, c, 0:1], y[:, c:c + 1],
                                               ALU.subtract, ALU.mult)
                if c % NC == NC - 1:
                    last.then_inc(fin_ready, 1)


def rope_tables():
    import numpy as np
    pos = np.arange(S, dtype=np.float32)
    rates = (np.float32(10000.0) ** (-(np.float32(2.0) * np.arange(DK // 2, dtype=np.float32)) / np.float32(DK))).astype(np.float32)
    ang = (pos[:, None] * rates[None, :]).astype(np.float32)
    cos, sin = np.cos(ang).astype(np.float32), np.sin(ang).astype(np.float32)
    row = np.arange(P) % DK
    sign = np.where(row % 2 == 0, -1.0, 1.0).astype(np.float32)
    return np.ascontiguousarray(cos[:, row // 2].T), np.ascontiguousarray(sin[:, row // 2].T * sign[:, None])


def kernel(**inputs):
    import numpy as np
    import concourse.bacc as bacc
    from concourse.bass_utils import run_bass_kernel_spmd

    x = np.asarray(inputs["L0_attn_x"])
    flat = x.reshape(TOK, D)
    swap = np.arange(D) ^ 1
    g = {k: np.asarray(inputs["L0_attn_" + k]) for k in ("Wq", "Wk", "Wv", "Wo")}
    f = {k: np.asarray(inputs["L0_ffn_" + k]) for k in ("gate_weight", "W1", "b1", "W2", "b2", "Ws1", "bs1", "Ws2", "bs2")}
    w1 = np.concatenate([f["Ws1"][None], f["W1"]], 0).transpose(1, 0, 2).reshape(D, NX * F)
    w2 = np.concatenate([f["Ws2"][None], f["W2"]], 0).reshape(NX, NF, P, D).transpose(2, 0, 1, 3).reshape(P, NX * F)
    b1 = np.concatenate([f["bs1"][None], f["b1"]], 0).reshape(NX * NF, P).T
    b2 = np.concatenate([f["bs2"][None], f["b2"]], 0).T
    cos, sin = rope_tables()
    selo = np.zeros((P, 36), np.float32)
    for j in range(4):
        for c in range(9):
            selo[32 * j + c, 9 * j + c] = 1.0
    sele = np.zeros((NE, NE, P), np.float32)
    for e in range(NE):
        sele[e, e] = 1.0
    arrays = dict(
        xT=flat.T, xr=flat, wqT=g["Wq"].T, wqsT=g["Wq"][swap].T, wkT=g["Wk"].T, wksT=g["Wk"][swap].T,
        wvT=g["Wv"].T, woT=g["Wo"].T, gwT=f["gate_weight"].T, w1=w1, w2=w2, b1=b1, b2=b2,
        cosT=cos, sinT=sin, ident=np.eye(P, dtype=np.float32), selo=selo, sele=sele.reshape(NE, NE * P),
    )
    arrays = {k: np.ascontiguousarray(v) for k, v in arrays.items()}
    nc = bacc.Bacc("TRN2", target_bir_lowering=False, num_devices=1)
    aps = {k: nc.dram_tensor(k, v.shape, mybir.dt.from_np(v.dtype), kind="ExternalInput").ap() for k, v in arrays.items()}
    out = nc.dram_tensor("y", (TOK, D), F32, kind="ExternalOutput").ap()
    moe_layer(nc, **aps, out=out)
    r = run_bass_kernel_spmd(nc, [arrays], core_ids=[0])
    return r.results[0]["y"].reshape(x.shape)
```

```python
from contextlib import ExitStack

import concourse.bass as bass
from concourse import mybir

ALU = mybir.AluOpType
ACT = mybir.ActivationFunctionType
AX = mybir.AxisListType
F32 = mybir.dt.float32
F32R = mybir.dt.float32r
BF16 = mybir.dt.bfloat16
U32 = mybir.dt.uint32
I32 = mybir.dt.int32

P = 128
NB = 8
S = 512
D = 128
NH = 16
DK = 8
NG = 4
NC = S // P
NE = 8
NX = NE + 1
F = 512
NF = F // P
TOK = NB * S
NCH = TOK // P
TOPK = 2 * TOK
EPS = 1e-5
SCALE = DK ** -0.5
NEG = -1e30
SEG = {0: 0, 1: 512, 3: 896, 2: 1024}
SEGW = 1280
BSTEPS = [(0,), (1, 3), (2,)]
MROW = 3 * P // 4
SUM_AT, HI_AT, LO_AT = ((11, 0), (12, 0)), ((1, 1), (2, 0)), ((2, 1), (3, 0))
MISC_USERS = (
    ("m1", 0, (1, 0)), ("v", 0, (4, 0)), ("m2", 0, (5, 0)), ("ot0", -1, (5, 1)), ("ot1", -1, (6, 1)), ("at", -1, (7, 1)),
    ("wo", -1, (8, 1)), ("m3", 0, (9, 0)), ("proj0", 2, (10, 0)), ("proj1", 2, (10, 1)), ("proj2", 2, (11, 0)),
    ("proj3", 2, (11, 1)), ("xt", -1, (12, 1)), ("m0", 1, (13, 0)), ("lg", -1, (14, 1)))
MISC_AT = {name: at for name, _, at in MISC_USERS}
V_AT, AT_AT, WO_AT, XT_AT, LG_AT = (MISC_AT[k] for k in ("v", "at", "wo", "xt", "lg"))
OT_AT = (MISC_AT["ot0"], MISC_AT["ot1"])
PROJ_AT = tuple(MISC_AT[f"proj{w}"] for w in range(4))
M_AT = {MISC_AT[f"m{g}"]: g for g in range(NG)}


LATE = (("wo", D), ("gw", NE), ("ident", P), ("selo", 36), ("heads", 4), ("minus", 1), ("b1", NX * NF), ("b2", NX))


def has(t, lag):
    return not isinstance(t, int) or 0 <= t + lag < NB


def later(t, lag):
    return not isinstance(t, int) or t + lag > 0


def group_after(t, g, ahead):
    lag, g = divmod(g + ahead, NG)
    return (lag, g) if has(t, lag) else None


def maxima_of(t, s, k):
    if (which := group_after(t, s // 4, 2)) is None:
        return None
    lag, g = which
    jp, i = divmod(2 * (s % 4) + k, NC)
    return lag, g, jp, i, 8 * g + 4 * jp + i


def rstd(nc, dve, var, work):
    v, h, y = work[:, 0, :], work[:, 1, :], work[:, 2, :]
    nc.vector.tensor_scalar(v, var, EPS, None, ALU.add)
    dve.drain()
    nc.vector.tensor_scalar(h.bitcast(U32), v.bitcast(U32), 1, None, ALU.logical_shift_right)
    dve.drain()
    nc.vector.tensor_scalar(y.bitcast(I32), h.bitcast(I32), -1.0, float(0x5F3759DF), ALU.mult, ALU.add)
    dve.drain()
    for _ in range(3):
        nc.vector.tensor_tensor(h, y, y, ALU.mult)
        dve.drain()
        nc.vector.tensor_tensor(h, h, v, ALU.mult)
        dve.drain()
        nc.vector.tensor_scalar(h, h, -0.5, 1.5, ALU.mult, ALU.add)
        dve.drain()
        nc.vector.tensor_tensor(y, y, h, ALU.mult)
        dve.drain()
    return y


def moe_layer(nc, xT, xr, early, late, w1, w2, sele, out):
    ctx = ExitStack()
    with ctx:
        def sb(name, shape, dt=F32):
            return ctx.enter_context(nc.sbuf_tensor(name, shape, dt))

        def sem(name):
            return ctx.enter_context(nc.semaphore(name))

        early_sb = sb("early_sb", [P, 5 * D + 2 * S])
        wproj = early_sb[:, 0:5 * D].rearrange("p (w d) -> p w d", w=5)
        cos_sb, sin_sb = early_sb[:, 5 * D:5 * D + S], early_sb[:, 5 * D + S:]
        late_sb = sb("late_sb", [P, sum(w for _, w in LATE)])
        wo_sb, gw_sb, id_sb, selo_sb, heads, minus, b1_sb, b2_sb = (
            late_sb[:, sum(w for _, w in LATE[:k]):sum(w for _, w in LATE[:k + 1])] for k in range(len(LATE)))
        sele_f = sb("sele_f", [NE, NE * P])
        x1 = sb("x1", [P, NCH, D])
        x1h = sb("x1h", [P, TOK], F32R)
        x1l = sb("x1l", [P, TOK], F32R)
        score = sb("score", [P, NCH, NE])
        loaded, loaded_late = sem("loaded"), sem("loaded_late")
        attention(nc, locals())
        experts(nc, locals())


def attention(nc, kept):
    (xT, xr, early, late, sele, early_sb, late_sb, sele_f, wproj, wo_sb, gw_sb, cos_sb, sin_sb, id_sb, selo_sb, heads, minus,
     x1, x1h, x1l, score, loaded, loaded_late, out) = (kept[k] for k in (
         "xT", "xr", "early", "late", "sele", "early_sb", "late_sb", "sele_f", "wproj", "wo_sb", "gw_sb", "cos_sb", "sin_sb",
         "id_sb", "selo_sb", "heads", "minus", "x1", "x1h", "x1l", "score", "loaded", "loaded_late", "out"))
    ctx = ExitStack()
    with ctx:
        def sb(name, shape, dt=F32):
            return ctx.enter_context(nc.sbuf_tensor(name, shape, dt))

        def sem(name):
            return ctx.enter_context(nc.semaphore(name))

        idb = sb("idb", [P, P], BF16)
        maskb = sb("maskb", [P, P], BF16)
        xq = sb("xq", [P, S])
        xv = sb("xv", [P, S])
        xres = sb("xres", [P, NC, D])
        rot = sb("rot", [P, 2, S])
        rsum = sb("rsum", [P, 2, S])
        den = sb("den", [P, 4, S], F32R)
        qk = sb("qk", [P, NG + 2, S], F32R)
        km = sb("km", [P, NG, 4, S], F32R)
        idr = sb("idr", [P, P], F32R)
        vaug = sb("vaug", [P, NC, NH, 32])
        pexp = sb("pexp", [P, 2, 4, SEGW])
        oT = sb("oT", [P, NG, S])
        rmax = sb("rmax", [P, 2, NC, 4])
        rmax2 = sb("rmax2", [P, NC, P], F32R)
        rec = sb("rec", [P, 2, NH])
        attn = sb("attn", [P, NC, D])
        attnT = sb("attnT", [P, S])
        xn = sb("xn", [P, NC, D])
        res = sb("res", [P, NC, D])
        bst = sb("bst", [P, NC, 6])
        bag = sb("bag", [P, NC, 2])
        nw = sb("nw", [P, 4, NC])
        x1T = sb("x1T", [P, S])
        lg = sb("lg", [P, NC, NE])
        lsm = sb("lsm", [P, 2, NC])
        ps = ctx.enter_context(nc.psum_tensor("ps", [P, 8, 512], F32))
        MISC = 7

        ready, stacks_ready = sem("ready"), sem("stacks_ready")
        xq_in, xv_in, xr_in = sem("xq_in"), sem("xv_in"), sem("xr_in")
        proj_done = sem("proj_done")
        rope_mul = sem("rope_mul")
        rope_sum = sem("rope_sum")
        rope_hi = sem("rope_hi")
        rope_lo = sem("rope_lo")
        fill = [sem(f"fill{g}") for g in range(NG)]
        zeroed = sem("zeroed")
        km_dve, km_act = sem("km_dve"), sem("km_act")
        m_split = sem("m_split")
        m_tr = sem("m_tr")
        m_out = sem("m_out")
        a_done = sem("a_done")
        a_max = sem("a_max")
        b_done = sem("b_done")
        b_exp = sem("b_exp")
        p_masked = sem("p_masked")
        pv_done = sem("pv_done")
        o_out = sem("o_out")
        v_done, v_out = sem("v_done"), sem("v_out")
        ot_done, ot_out = sem("ot_done"), sem("ot_out")
        at_done, at_out = sem("at_done"), sem("at_out")
        wo_done, r_done, n_done = sem("wo_done"), sem("r_done"), sem("n_done")
        xt_done, xt_out, x1_kept = sem("xt_done"), sem("xt_out"), sem("x1_kept")
        x1l_done = sem("x1l_done")
        lg_done, lg_sub, lg_exp, lg_fin = sem("lg_done"), sem("lg_sub"), sem("lg_exp"), sem("lg_fin")

        sp_step, pool_step = sem("sp_step"), sem("pool_step")
        block = ctx.enter_context(nc.Block())

        def bodies(eng, body):
            for t in range(-2, 2):
                body(t)
            with eng.Fori(2, NB - 2) as t:
                body(t)
            for t in range(NB - 2, NB + 1):
                body(t)

        @block.sync
        def _(sp):
            sp.dma_start(early_sb[:], early).then_inc(loaded, 16)
            sp.dma_start(xq[:], xT[:, 0:S]).then_inc(xq_in, 16)
            sp.dma_start(late_sb[:], late).then_inc(loaded_late, 16)
            sp.dma_start(sele_f[:], sele).then_inc(loaded_late, 16)

            def after(signal, value):
                sp.wait_ge(signal, value)
                sp.sem_inc(sp_step, 1)

            def body(t):
                for g in range(NG):
                    if (which := group_after(t, g, 3)) is not None:
                        lag, to = which
                        if later(t, lag):
                            after(b_done, 48 * (t + lag - 1) + 12 * to + 12)
                        if later(t, lag) or to >= 2:
                            after(km_dve, 8 * (t + lag) + 2 * to - 2)
                            after(km_act, 8 * (t + lag) + 2 * to - 2)
                        elif to == 0:
                            after(stacks_ready, 1)
                        if to == 0:
                            after(rope_lo, 2 * (t + lag + 1))
                        rows = slice(32 * to, 32 * to + 32)
                        step = NG + to % 2 - to
                        for r, (first, apart) in enumerate(((1, 1), (0, 2), (1, 2))):
                            sp.dma_start(qk[32 * r:32 * r + 32, to:to + step + 1:step, :].bitcast(F32),
                                         den[rows, first:first + apart + 1:apart, :].bitcast(F32)).then_inc(fill[to], 16)
                    if g == 0 and has(t, 2) and later(t, 2):
                        after(proj_done, 4 * (t + 2))
                        sp.dma_start(xq[:], xT[:, bass.ds((t + 2) * S, S)]).then_inc(xq_in, 16)
                    if g == 0 and has(t, -1):
                        if later(t, -1):
                            after(r_done, t - 1)
                        sp.dma_start(xres[:], xr[bass.ds((t - 1) * S, S), :].rearrange("(c p) d -> p c d", p=P)).then_inc(xr_in, 16)
                    if g == 1 and has(t, 1):
                        if later(t, 1):
                            after(v_done, t + 1)
                        sp.dma_start(xv[:], xT[:, bass.ds((t + 1) * S, S)]).then_inc(xv_in, 16)
                if has(t, -1):
                    after(n_done, t)
                    sp.dma_start(x1[:, bass.ds((t - 1) * NC, NC), :], xn[:]).then_inc(x1_kept, 16)

            bodies(nc.sync, body)

        @block.gpsimd
        def _(pool):
            nc.gpsimd.memset(idb[:], 0.0)
            nc.gpsimd.memset(maskb[:], 0.0)
            nc.gpsimd.memset(rmax2[:].bitcast(F32), 0.0)
            nc.gpsimd.memset(vaug[:], 0.0)
            nc.gpsimd.memset(qk[:, 0:NG, :].bitcast(F32), 0.0)
            pool.drain()
            nc.gpsimd.affine_select(out=idb[:], in_=idb[:], compare_op=ALU.not_equal, fill=1.0, base=0,
                                    pattern=[[-1, P]], channel_multiplier=1)
            nc.gpsimd.memset(vaug[:, :, :, 8:9], 1.0)
            nc.gpsimd.affine_select(out=maskb[:], in_=maskb[:], compare_op=ALU.is_ge, fill=NEG, base=0,
                                    pattern=[[-1, P]], channel_multiplier=1).then_inc(ready, 1)

            def place(t, at):
                s, k = at
                g, u = divmod(s, 4)
                if has(t, 0) and u == 0 and k == 0 and g > 0:
                    mask(t, g - 1)
                if has(t, 0) and at == (15, 1):
                    mask(t, NG - 1)
                if has(t, 2) and at in SUM_AT:
                    n, w = t + 2, SUM_AT.index(at)
                    pool.wait_ge(rope_mul, 4 * n + 2 * w + 2)
                    nc.gpsimd.tensor_tensor(rsum[:, w, :], rot[:, 0, :], rot[:, 1, :], ALU.add).then_inc(rope_sum, 1)
                if has(t, 1) and at in LO_AT:
                    n, w = t + 1, LO_AT.index(at)
                    pool.wait_ge(rope_hi, 2 * n + w + 1)
                    nc.gpsimd.tensor_tensor(den[:, 3 * w, :], rsum[:, w, :], den[:, 1 + w, :].bitcast(F32),
                                            ALU.subtract).then_inc(rope_lo, 1)
                if u == 1 and k == 0 and (which := group_after(t, g, 3)) is not None and later(t, which[0]):
                    lag, to = which
                    pool.wait_ge(b_done, 48 * (t + lag - 1) + 12 * to + 12)
                    pool.sem_inc(pool_step, 1)
                    pool.drain()
                    nc.gpsimd.memset(qk[MROW:P, to, :].bitcast(F32), 0.0).then_inc(zeroed, 1)
                    pool.drain()
                if has(t, -1) and at == (XT_AT[0] + 1, 0):
                    pool.wait_ge(xt_out, 2 * t)
                    nc.gpsimd.tensor_tensor(x1l[:, bass.ds((t - 1) * S, S)], x1T[:],
                                            x1h[:, bass.ds((t - 1) * S, S)].bitcast(F32), ALU.subtract).then_inc(x1l_done, 1)
            def mask(t, g):
                pool.wait_ge(b_exp, 48 * t + 12 * g + 12)
                pool.sem_inc(pool_step, 1)
                for i in range(NC):
                    blk = pexp[:, g % 2, :, SEG[i]:SEG[i] + P]
                    nc.gpsimd.affine_select(out=blk, in_=blk, compare_op=ALU.is_ge, fill=0.0, base=0,
                                            pattern=[[0, 4], [1, P]], channel_multiplier=-1).then_inc(p_masked, 1)

            def body(t):
                for s in range(16):
                    for k in range(2):
                        place(t, (s, k))

            bodies(nc.gpsimd, body)

        @block.scalar
        def _(act):
            def exponentials(t, s, k):
                g, u = divmod(s, 4)
                act.wait_ge(b_done, 48 * t + 3 * s + k + 1)
                if k == 0 and u == 0 and (g > 1 or later(t, 0)):
                    act.wait_ge(pv_done, 4 * t + g - 1)
                blocks = BSTEPS[k]
                first, width = SEG[blocks[0]], sum(S - P * i for i in blocks)
                nc.scalar.activation(pexp[:, g % 2, u, first:first + width], ps[:, 4 + (3 * s + k) % 2, 0:width],
                                     ACT.Exp, scale=SCALE).then_inc(b_exp, 1)

            def place(t, at):
                s, k = at
                if has(t, 1) and at in HI_AT:
                    n, w = t + 1, HI_AT.index(at)
                    act.wait_ge(rope_sum, 2 * n + w + 1)
                    if w == 0 and later(t, 1):
                        for g in range(NG):
                            act.wait_ge(fill[g], 48 * n)
                    nc.scalar.activation(den[:, 1 + w, :], rsum[:, w, :], ACT.Copy).then_inc(rope_hi, 1)
                if s % 4 in (2, 3) and k == 0 and (which := group_after(t, s // 4, 3)) is not None:
                    lag, g = which
                    j = 2 * (s % 4) - 3
                    act.wait_ge(fill[g], 48 * (t + lag + 1))
                    nc.scalar.activation(km[:, g, j, :], qk[:, NG + g % 2, :].bitcast(F32), ACT.Copy,
                                         scale=heads[:, j:j + 1]).then_inc(km_act, 1)
                if has(t, 0) and at == V_AT:
                    act.wait_ge(v_done, t + 1)
                    if later(t, 0):
                        act.wait_ge(pv_done, 4 * t)
                    else:
                        act.wait_ge(ready, 1)
                    nc.scalar.activation(vaug[:, :, :, 0:DK], ps[:, MISC, :].rearrange("p (c h d) -> p c h d", c=NC, d=DK),
                                         ACT.Copy).then_inc(v_out, 1)
                if has(t, -1) and at == AT_AT:
                    act.wait_ge(at_done, t)
                    nc.scalar.activation(attnT[:], ps[:, MISC, :], ACT.Copy).then_inc(at_out, 1)
                if has(t, -1) and at == XT_AT:
                    act.wait_ge(xt_done, t)
                    if later(t, -1):
                        act.wait_ge(x1l_done, t - 1)
                    nc.scalar.activation(x1T[:], ps[:, MISC, :], ACT.Copy).then_inc(xt_out, 1)
                    nc.scalar.activation(x1h[:, bass.ds((t - 1) * S, S)], ps[:, MISC, :], ACT.Copy).then_inc(xt_out, 1)
                if has(t, -1) and at == LG_AT:
                    act.wait_ge(lg_sub, t)
                    nc.scalar.activation(lg[:], lg[:], ACT.Exp).then_inc(lg_exp, 1)
                if at in M_AT and has(t, int(M_AT[at] == 0)):
                    g = M_AT[at]
                    count = 4 * (t + (g == 0)) + g + 1
                    act.wait_ge(m_tr, count)
                    nc.scalar.activation(qk[MROW:P, g, :], ps[MROW:P, MISC, :], ACT.Copy).then_inc(m_out, 1)

            def body(t):
                for s in range(16):
                    g, u = divmod(s, 4)
                    if u == 0 and g > 1 and has(t, 0):
                        act.wait_ge(pv_done, 4 * t + g - 1)
                        if g == 2 and later(t, 0):
                            act.wait_ge(ot_done, 2 * t)
                        nc.scalar.activation(oT[:, g - 2, :], ps[:, 6, :], ACT.Copy).then_inc(o_out, 1)
                    if u == 0 and g < 2 and has(t, -1):
                        act.wait_ge(pv_done, 4 * t + g - 1)
                        nc.scalar.activation(oT[:, 2 + g, :], ps[:, 6, :], ACT.Copy).then_inc(o_out, 1)
                    for k in range(3):
                        if has(t, 0):
                            exponentials(t, s, k)
                        if k < 2:
                            place(t, (s, k))

            bodies(nc.scalar, body)

        @block.tensor
        def _(pe):
            pe.wait_ge(loaded, 16)

            def maxima(t, s, k):
                if (step := maxima_of(t, s, k)) is None:
                    return
                lag, g, jp, i, number = step
                if i == 0:
                    pe.wait_ge(km_dve, 8 * (t + lag) + 2 * g + jp + 1)
                    pe.wait_ge(km_act, 8 * (t + lag) + 2 * g + jp + 1)
                    if jp == 0 and later(t, lag):
                        pe.wait_ge(zeroed, 4 * (t + lag - 1) + g + 1)
                if later(t, lag) or number >= 2:
                    pe.wait_ge(a_max, 32 * (t + lag) + number - 1)
                bank = 2 * (number % 2)
                for j in range(2):
                    nc.tensor.matmul(ps[:, bank + j, 0:P * (i + 1)], qk[:, g, P * i:P * (i + 1)],
                                     km[:, g, 2 * jp + j, 0:P * (i + 1)], start=True, stop=False)
                for j in range(2):
                    last = nc.tensor.matmul(ps[:, bank + j, P * i:P * (i + 1)], idb[:], maskb[:], start=False, stop=True)
                last.then_inc(a_done, 1)

            def exponents(t, s, k):
                g, u = divmod(s, 4)
                if u == 0 and k == 0:
                    pe.wait_ge(m_out, 4 * t + g + 1)
                step = 3 * s + k
                if later(t, 0) or step >= 2:
                    pe.wait_ge(b_exp, 48 * t + step - 1)
                at = 0
                for i in BSTEPS[k]:
                    last = nc.tensor.matmul(ps[:, 4 + step % 2, at:at + S - P * i], km[:, g, u, P * i:P * (i + 1)],
                                            qk[:, g, P * i:S], start=(at == 0), stop=True, skip_group_check=True)
                    at += S - P * i
                last.then_inc(b_done, 1)

            def values(t, g, i):
                if i == 0:
                    pe.wait_ge(p_masked, 16 * t + 4 * g + 4)
                    if g > 0 or later(t, 0):
                        pe.wait_ge(o_out, 4 * t + g)
                    if g == 0:
                        pe.wait_ge(v_out, t + 1)
                for j in range(4):
                    last = nc.tensor.matmul(ps[32 * j:32 * j + 32, 6, P * i:S], vaug[:, i, 4 * g + j, :],
                                            pexp[:, g % 2, j, SEG[i]:SEG[i] + S - P * i], start=(i == 0), stop=(i == NC - 1),
                                            skip_group_check=True)
                if i == NC - 1:
                    last.then_inc(pv_done, 1)

            def wait_misc_free(t, at):
                users = [(name, t + lag) for name, lag, _ in MISC_USERS if has(t, lag)]
                before = [(name, t + lag - 1) for name, lag, _ in MISC_USERS if has(t, lag - 1)]
                me = next(k for k, (name, _) in enumerate(users) if MISC_AT[name] == at)
                past = before + users[:me]
                if not past:
                    return
                name, n = past[-1]
                if name[0] == "m":
                    pe.wait_ge(m_out, 4 * n + int(name[1]) + 1)
                elif name == "v":
                    pe.wait_ge(v_out, n + 1)
                elif name[:2] == "ot":
                    pe.wait_ge(ot_out, 2 * n + int(name[2]) + 1)
                elif name == "at":
                    pe.wait_ge(at_out, n + 1)
                elif name == "wo":
                    pe.wait_ge(r_done, n + 1)
                elif name[:4] == "proj":
                    pe.wait_ge(rope_mul, 4 * n + int(name[4]) + 1)
                elif name == "xt":
                    pe.wait_ge(xt_out, 2 * n + 2)
                else:
                    pe.wait_ge(lg_sub, n + 1)

            def place(t, at):
                if has(t, 2) and at in PROJ_AT:
                    n, w = t + 2, PROJ_AT.index(at)
                    if w == 0:
                        pe.wait_ge(xq_in, 16 * (n + 1))
                    wait_misc_free(t, at)
                    nc.tensor.matmul(ps[:, MISC, :], wproj[:, w, :], xq[:], start=True, stop=True).then_inc(proj_done, 1)
                if at in M_AT and has(t, int(M_AT[at] == 0)):
                    g = M_AT[at]
                    wait_misc_free(t, at)
                    pe.wait_ge(m_split, 4 * (t + (g == 0)) + g + 1)
                    for c in range(NC):
                        last = nc.tensor.matmul(ps[:, MISC, P * c:P * (c + 1)], rmax2[:, c, :], idr[:], start=True, stop=True)
                    last.then_inc(m_tr, 1)
                if has(t, 0) and at == V_AT:
                    wait_misc_free(t, at)
                    pe.wait_ge(xv_in, 16 * (t + 1))
                    for c in range(NC):
                        last = nc.tensor.matmul(ps[:, MISC, P * c:P * (c + 1)], xv[:, P * c:P * (c + 1)], wproj[:, 4, :],
                                                start=True, stop=True)
                    last.then_inc(v_done, 1)
                if has(t, -1) and at in OT_AT:
                    half = OT_AT.index(at)
                    wait_misc_free(t, at)
                    if half == 0:
                        pe.wait_ge(o_out, 4 * t)
                    for c in range(2):
                        for g in range(NG):
                            to = (c * NG + g) * 36
                            last = nc.tensor.matmul(ps[:, MISC, to:to + 36], oT[:, g, P * (2 * half + c):P * (2 * half + c + 1)],
                                                    selo_sb, start=True, stop=True)
                    last.then_inc(ot_done, 1)
                if has(t, -1) and at == AT_AT:
                    wait_misc_free(t, at)
                    for c in range(NC):
                        last = nc.tensor.transpose(ps[:, MISC, P * c:P * (c + 1)], attn[:, c, :], id_sb)
                    last.then_inc(at_done, 1)
                if has(t, -1) and at == WO_AT:
                    wait_misc_free(t, at)
                    for c in range(NC):
                        last = nc.tensor.matmul(ps[:, MISC, P * c:P * (c + 1)], attnT[:, P * c:P * (c + 1)], wo_sb,
                                                start=True, stop=True)
                    last.then_inc(wo_done, 1)
                if has(t, -1) and at == XT_AT:
                    wait_misc_free(t, at)
                    pe.wait_ge(n_done, t)
                    for c in range(NC):
                        last = nc.tensor.transpose(ps[:, MISC, P * c:P * (c + 1)], xn[:, c, :], id_sb)
                    last.then_inc(xt_done, 1)
                if has(t, -1) and at == LG_AT:
                    wait_misc_free(t, at)
                    pe.wait_ge(xt_out, 2 * t)
                    for c in range(NC):
                        last = nc.tensor.matmul(ps[:, MISC, NE * c:NE * (c + 1)], x1T[:, P * c:P * (c + 1)], gw_sb,
                                                start=True, stop=True)
                    last.then_inc(lg_done, 1)

            def body(t):
                for s in range(16):
                    g, u = divmod(s, 4)
                    for k in range(3):
                        if has(t, 0):
                            exponents(t, s, k)
                        if k < 2:
                            maxima(t, s, k)
                            place(t, (s, k))
                    if g > 0 and has(t, 0):
                        values(t, g - 1, u)
                    if g == 0 and has(t, -1):
                        values(t - 1, NG - 1, u)

            bodies(nc.tensor, body)

        @block.vector
        def _(dve):
            dve.wait_ge(loaded, 16)
            dve.wait_ge(ready, 1)
            dve.wait_ge(loaded_late, 32)
            nc.vector.tensor_copy(idr[:], id_sb)
            nc.vector.tensor_copy(qk[:, NG:, :].rearrange("p g n -> p (g n)"), minus.to_broadcast([P, 2 * S]))\
              .then_inc(stacks_ready, 1)

            def maxima(t, s, k):
                if (step := maxima_of(t, s, k)) is None:
                    return
                lag, g, jp, i, number = step
                dve.wait_ge(a_done, 32 * (t + lag) + number + 1)
                bank = 2 * (number % 2)
                nc.vector.tensor_reduce(rmax[:, g % 2, i, 2 * jp:2 * jp + 2],
                                        ps[:, bank:bank + 2, 0:P * (i + 1)], AX.X, ALU.max).then_inc(a_max, 1)

            def split_maxima(t, g, ahead):
                if (which := group_after(t, g, ahead)) is None:
                    return
                lag, g = which
                dve.drain()
                if later(t, lag) or g > 0:
                    dve.wait_ge(m_tr, 4 * (t + lag) + g)
                nc.vector.tensor_copy(rmax2[:, :, MROW:MROW + 4], rmax[:, g % 2, :, :])
                dve.drain()
                nc.vector.tensor_tensor(rmax2[:, :, MROW + 4:MROW + 8], rmax[:, g % 2, :, :],
                                        rmax2[:, :, MROW:MROW + 4].bitcast(F32), ALU.subtract).then_inc(m_split, 1)

            def place(t, at):
                s, k = at
                if s % 4 in (2, 3) and k == 0 and (which := group_after(t, s // 4, 3)) is not None:
                    lag, g = which
                    j = 2 * (s % 4) - 4
                    dve.wait_ge(fill[g], 48 * (t + lag + 1))
                    nc.vector.tensor_scalar(km[:, g, j, :], qk[:, NG + g % 2, :].bitcast(F32), heads[:, j:j + 1], None,
                                            ALU.mult).then_inc(km_dve, 1)
                if has(t, 2) and at in PROJ_AT:
                    n, w = t + 2, PROJ_AT.index(at)
                    dve.wait_ge(proj_done, 4 * n + w + 1)
                    if w % 2 == 0 and (w == 2 or later(t, 2)):
                        dve.wait_ge(rope_sum, 2 * n + w // 2)
                    nc.vector.tensor_tensor(rot[:, w % 2, :], ps[:, MISC, :], cos_sb if w % 2 == 0 else sin_sb,
                                            ALU.mult).then_inc(rope_mul, 1)
                if has(t, -1) and at in OT_AT:
                    half = OT_AT.index(at)
                    dve.wait_ge(ot_done, 2 * (t - 1) + half + 1)
                    if half == 0 and later(t, -1):
                        dve.wait_ge(at_done, t - 1)
                    sums = ps[:, MISC, 0:8 * 36].rearrange("p (c h k) -> p c h k", c=2, k=9)
                    nc.vector.reciprocal(rec[:], sums[:, :, :, 8])
                    dve.drain()
                    nc.vector.tensor_tensor(attn[:, 2 * half:2 * half + 2, :].rearrange("p c (h d) -> p c h d", d=DK),
                                            sums[:, :, :, 0:DK], rec[:].unsqueeze(3).to_broadcast([P, 2, NH, DK]),
                                            ALU.mult).then_inc(ot_out, 1)
                    dve.drain()
                if has(t, -1) and at == WO_AT:
                    dve.wait_ge(wo_done, t)
                    dve.wait_ge(xr_in, 16 * t)
                    nc.vector.tensor_tensor(res[:].rearrange("p c d -> p (c d)"), ps[:, MISC, :],
                                            xres[:].rearrange("p c d -> p (c d)"), ALU.add).then_inc(r_done, 1)
                    dve.drain()
                    for c in range(NC):
                        nc.vector.bn_stats(bst[:, c, :], res[:, c, :])
                    dve.drain()
                    for c in range(NC):
                        nc.vector.bn_aggr(bag[:, c, :], bst[:, c, :])
                    dve.drain()
                    y = rstd(nc, dve, bag[:, :, 1], nw)
                    if later(t, -1):
                        dve.wait_ge(xt_done, t - 1)
                        dve.wait_ge(x1_kept, 16 * (t - 1))
                    for c in range(NC):
                        last = nc.vector.tensor_scalar(xn[:, c, :], res[:, c, :], bag[:, c, 0:1], y[:, c:c + 1],
                                                       ALU.subtract, ALU.mult)
                    last.then_inc(n_done, 1)
                if has(t, -1) and at == LG_AT:
                    dve.wait_ge(lg_done, t)
                    logits = ps[:, MISC, 0:NC * NE].rearrange("p (c e) -> p c e", e=NE)
                    nc.vector.tensor_reduce(lsm[:, 0, :], logits, AX.X, ALU.max)
                    dve.drain()
                    nc.vector.tensor_tensor(lg[:], logits, lsm[:, 0, :].unsqueeze(2).to_broadcast([P, NC, NE]),
                                            ALU.subtract).then_inc(lg_sub, 1)
                    dve.wait_ge(lg_exp, t)
                    nc.vector.tensor_reduce(lsm[:, 1, :], lg[:], AX.X, ALU.add)
                    dve.drain()
                    nc.vector.reciprocal(lsm[:, 0, :], lsm[:, 1, :])
                    dve.drain()
                    dst = score[:, bass.ds((t - 1) * NC, NC), :]
                    nc.vector.tensor_tensor(dst, lg[:], lsm[:, 0, :].unsqueeze(2).to_broadcast([P, NC, NE]),
                                            ALU.mult).then_inc(lg_fin, 1)
                    dve.drain()

            def body(t):
                for s in range(16):
                    if s % 4 == 0:
                        split_maxima(t, s // 4, 1)
                    for k in range(2):
                        maxima(t, s, k)
                        place(t, (s, k))

            bodies(nc.vector, body)


def experts(nc, kept):
    (w1, w2, sele_f, id_sb, b1_sb, b2_sb, x1, x1h, x1l, score, out) = (
        kept[k] for k in ("w1", "w2", "sele_f", "id_sb", "b1_sb", "b2_sb", "x1", "x1h", "x1l", "score", "out"))
    NT = TOK // S
    BITS = 30
    NS = NCH * NE
    ctx = ExitStack()
    with ctx:
        def sb(name, shape, dt=F32):
            return ctx.enter_context(nc.sbuf_tensor(name, shape, dt))

        def sem(name):
            return ctx.enter_context(nc.semaphore(name))

        ones = sb("ones", [P, P])
        before = sb("before", [P, P])
        ones_row = sb("ones_row", [P, NS])
        thr, trial, cand, need = (sb(n, [P, 1]) for n in ("thr", "trial", "cand", "need"))
        count = sb("count", [P, 1])
        hit = sb("hit", [P, NS])
        equal = sb("equal", [P, NE, NCH])
        rank = sb("rank", [P, NS])
        upto = sb("upto", [P, NS])
        gate = sb("gate", [P, NCH, NE])
        gT_hi = sb("gT_hi", [NE, TOK], F32R)
        gT_lo = sb("gT_lo", [NE, TOK], F32R)
        w_stage = sb("w_stage", [P, 2, F])
        b1_cur = sb("b1_cur", [P, 2, NF])
        sel_cur = sb("sel_cur", [NE, 2, P], F32R)
        w1h, w1l, w2h, w2l = (sb(n, [P, 2, F], F32R) for n in ("w1h", "w1l", "w2h", "w2l"))
        acc = sb("acc", [P, TOK])
        h = sb("h", [P, NF, S])
        hh = sb("hh", [P, 2, NF, S], F32R)
        hl = sb("hl", [P, 2, NF, S], F32R)
        gbc = sb("gbc", [P, 2, S])
        part = sb("part", [P, 2, S])
        res2 = sb("res2", [P, NCH, D])
        bst2 = sb("bst2", [P, NCH, 6])
        bag2 = sb("bag2", [P, NCH, 2])
        nw2 = sb("nw2", [P, 3, NCH])
        pe_ps = ctx.enter_context(nc.psum_tensor("pe_ps", [P, 8, 512], F32))

        built = sem("built")
        counted, totalled = sem("counted"), sem("totalled")
        eq_done, eq_sums, gate_done = sem("eq_done"), sem("eq_sums"), sem("gate_done")
        gt_tr, gt_hi, gt_lo = sem("gt_tr"), sem("gt_hi"), sem("gt_lo")
        w_in, w_split = sem("w_in"), sem("w_split")
        up_done, gelu_done = sem("up_done"), sem("gelu_done")
        hh_done, hl_done = sem("hh_done"), sem("hl_done")
        down_done, y_done = sem("down_done"), sem("y_done")
        g_done, g_out, acc_done = sem("g_done"), sem("g_out"), sem("acc_done")
        fin_tr, fin_in, fin_ready, stored = sem("fin_tr"), sem("fin_in"), sem("fin_ready"), sem("stored")
        sp_turn = sem("sp_turn")
        block = ctx.enter_context(nc.Block())

        def after(eng, signal, value):
            if not isinstance(value, int) or value > 0:
                eng.wait_ge(signal, value)

        def all_experts(eng, expert):
            expert(0, 0)
            expert(1, 1)
            with eng.Fori(0, (NE - 2) // 2) as i:
                expert(2 * i + 2, 0)
                expert(2 * i + 3, 1)
            expert(NE, 0)

        @block.sync
        def _(sp):
            def load(e):
                sp.dma_start(w_stage[:, 0, :], w1[:, bass.ds(e * F, F)]).then_inc(w_in, 16)
                sp.dma_start(w_stage[:, 1, :], w2[:, bass.ds(e * F, F)]).then_inc(w_in, 16)

            load(0)

            def expert(e, buf):
                if isinstance(e, int) and e == NE:
                    return
                sp.wait_ge(w_split, e + 1)
                sp.sem_inc(sp_turn, 1)
                load(e + 1)

            all_experts(nc.sync, expert)
            for c in range(8):
                sp.wait_ge(fin_ready, c + 1)
                sp.dma_start(out[c * S:(c + 1) * S, :].rearrange("(c p) d -> p c d", p=P), res2[:, NC * c:NC * c + NC, :])\
                  .then_inc(stored, 16)
            sp.wait_ge(stored, 16 * 8)

        @block.gpsimd
        def _(pool):
            nc.gpsimd.memset(ones[:], 1.0)
            nc.gpsimd.memset(ones_row[:], 1.0)
            nc.gpsimd.memset(before[:], 1.0)
            pool.drain()
            nc.gpsimd.affine_select(out=before[:], in_=before[:], compare_op=ALU.is_gt, fill=0.0, base=0,
                                    pattern=[[1, P]], channel_multiplier=-1).then_inc(built, 1)

            def expert(e, buf):
                if isinstance(e, int) and e == 0:
                    return
                for t in range(NT):
                    u = NT * e + t
                    pool.wait_ge(y_done, u + 1)
                    nc.gpsimd.tensor_tensor(acc[:, t * S:(t + 1) * S], acc[:, t * S:(t + 1) * S], part[:, t % 2, :],
                                            ALU.add).then_inc(acc_done, 1)

            all_experts(nc.gpsimd, expert)

        @block.scalar
        def _(act):
            for k in range(NT):
                act.wait_ge(gt_tr, k + 1)
                nc.scalar.activation(gT_hi[:, k * S:(k + 1) * S], pe_ps[0:NE, k, :], ACT.Copy).then_inc(gt_hi, 1)

            def expert(e, buf):
                for t in range(NT):
                    u = NT * e + t
                    for f in range(NF):
                        act.wait_ge(up_done, NF * u + f + 1)
                        after(act, hl_done, NF * (u - 1) + f + 1)
                        nc.scalar.activation(h[:, f, :], pe_ps[:, f, :], ACT.Gelu_apprx_tanh,
                                             bias=b1_cur[:, buf, f:f + 1]).then_inc(gelu_done, 1)
                    if not isinstance(e, int) or e > 0:
                        act.wait_ge(g_done, u - NT + 1)
                        act.wait_ge(y_done, u - 1)
                        nc.scalar.activation(gbc[:, t % 2, :], pe_ps[:, 6, :], ACT.Copy).then_inc(g_out, 1)

            all_experts(nc.scalar, expert)

        @block.tensor
        def _(pe):
            pe.wait_ge(built, 1)
            for k in range(BITS + 1):
                pe.wait_ge(counted, k + 1)
                nc.tensor.matmul(pe_ps[:, 7, 0:1], ones[:], count[:], start=True, stop=True).then_inc(totalled, 1)
            pe.wait_ge(eq_done, 1)
            nc.tensor.matmul(pe_ps[:, 5, 0:NS], ones[:], equal[:].rearrange("p e c -> p (e c)"), start=True, stop=True)
            nc.tensor.matmul(pe_ps[:, 6, 0:NS], before[:], equal[:].rearrange("p e c -> p (e c)"),
                             start=True, stop=True).then_inc(eq_sums, 1)
            pe.wait_ge(gate_done, 1)
            for k in range(NT):
                for c in range(NC):
                    last = nc.tensor.transpose(pe_ps[0:NE, k, P * c:P * (c + 1)], gate[:, NC * k + c, :], id_sb)
                last.then_inc(gt_tr, 1)
            pe.wait_ge(gt_lo, NT)

            def down(e, buf, t):
                u = NT * e + t
                after(pe, y_done, u - 1)
                n = 0
                for f in range(NF):
                    w = slice(P * f, P * (f + 1))
                    pe.wait_ge(hl_done, NF * u + f + 1)
                    for a, b in ((w2h, hh), (w2l, hh), (w2h, hl)):
                        last = nc.tensor.matmul(pe_ps[:, 4 + t % 2, :], a[:, buf, w], b[:, t % 2, f, :],
                                                start=(n == 0), stop=(n == 3 * NF - 1))
                        n += 1
                last.then_inc(down_done, 1)

            def final(t):
                pe.wait_ge(acc_done, NT * (NE - 1) + t + 1)
                after(pe, fin_in, t)
                for c in range(NC):
                    last = nc.tensor.transpose(pe_ps[:, 7, P * c:P * (c + 1)], acc[:, t * S + P * c:t * S + P * (c + 1)], id_sb)
                last.then_inc(fin_tr, 1)

            def expert(e, buf):
                pe.wait_ge(w_split, e + 1)
                for t in range(NT):
                    u = NT * e + t
                    for f in range(NF):
                        w = slice(P * f, P * (f + 1))
                        after(pe, gelu_done, NF * (u - 1) + f + 1)
                        xs = slice(t * S, (t + 1) * S)
                        for n, (a, b) in enumerate(((w1h, x1h), (w1l, x1h), (w1h, x1l))):
                            last = nc.tensor.matmul(pe_ps[:, f, :], a[:, buf, w], b[:, xs], start=(n == 0), stop=(n == 2))
                        last.then_inc(up_done, 1)
                    if not isinstance(e, int) or e > 0:
                        if not isinstance(e, int) or u > NT:
                            pe.wait_ge(g_out, u - NT)
                        nc.tensor.matmul(pe_ps[:, 6, :], sel_cur[:, buf, :], gT_hi[:, xs], start=True, stop=False)
                        nc.tensor.matmul(pe_ps[:, 6, :], sel_cur[:, buf, :], gT_lo[:, xs], start=False, stop=True)\
                          .then_inc(g_done, 1)
                    if t > 0:
                        down(e, buf, t - 1)
                    elif not isinstance(e, int) or e > 0:
                        down(e - 1, 1 - buf, NT - 1)
                    if isinstance(e, int) and e == NE and t >= 3:
                        final(t - 3)

            all_experts(nc.tensor, expert)
            down(NE, 0, NT - 1)
            for t in range(NT - 3, NT):
                final(t)

        @block.vector
        def _(dve):
            def split(e, buf):
                dve.wait_ge(w_in, 32 * (e + 1))
                for w, hi in ((0, w1h), (1, w2h)):
                    nc.vector.tensor_copy(hi[:, buf, :], w_stage[:, w, :])
                nc.vector.tensor_copy(b1_cur[:, buf, :], b1_sb[:, bass.ds(e * NF, NF)])
                if not isinstance(e, int) or e > 0:
                    nc.vector.tensor_copy(sel_cur[:, buf, :], sele_f[:, bass.ds((e - 1) * P, P)])
                dve.drain()
                for w, hi, lo in ((0, w1h, w1l), (1, w2h, w2l)):
                    last = nc.vector.tensor_tensor(lo[:, buf, :], w_stage[:, w, :], hi[:, buf, :].bitcast(F32), ALU.subtract)
                last.then_inc(w_split, 1)

            split(0, 0)
            dve.wait_ge(built, 1)
            flat = score[:].rearrange("p c e -> p (c e)")
            nc.vector.memset(thr[:].bitcast(U32), 0)
            dve.drain()
            for k in range(BITS):
                nc.vector.tensor_scalar(trial[:].bitcast(U32), thr[:].bitcast(U32), 1 << (BITS - 1 - k), None, ALU.bitwise_or)
                dve.drain()
                nc.vector.tensor_scalar(hit[:], flat, trial[:, 0:1], 0.0, ALU.is_ge, ALU.add, accum_out=count[:])\
                  .then_inc(counted, 1)
                dve.wait_ge(totalled, k + 1)
                nc.vector.scalar_tensor_tensor(cand[:], pe_ps[:, 7, 0:1], float(TOPK), trial[:], ALU.is_ge, ALU.mult)
                dve.drain()
                nc.vector.tensor_tensor(thr[:], thr[:], cand[:], ALU.max)
                dve.drain()
            nc.vector.tensor_scalar(hit[:], flat, thr[:, 0:1], 0.0, ALU.is_gt, ALU.add, accum_out=count[:]).then_inc(counted, 1)
            nc.vector.tensor_scalar(equal[:].rearrange("p e c -> p c e"), score[:], thr[:, 0:1], None, ALU.is_equal)\
              .then_inc(eq_done, 1)
            dve.wait_ge(totalled, BITS + 1)
            nc.vector.tensor_scalar(need[:], pe_ps[:, 7, 0:1], -1.0, float(TOPK), ALU.mult, ALU.add)
            dve.wait_ge(eq_sums, 1)
            nc.vector.tensor_tensor_scan(upto[:], ones_row[:], pe_ps[:, 5, 0:NS], 0.0, ALU.mult, ALU.add)
            dve.drain()
            nc.vector.tensor_tensor(upto[:], upto[:], pe_ps[:, 5, 0:NS], ALU.subtract)
            dve.drain()
            nc.vector.tensor_tensor(rank[:], upto[:], pe_ps[:, 6, 0:NS], ALU.add)
            dve.drain()
            nc.vector.scalar_tensor_tensor(upto[:], rank[:], need[:, 0:1], equal[:].rearrange("p e c -> p (e c)"),
                                           ALU.is_lt, ALU.mult)
            dve.drain()
            nc.vector.tensor_tensor(gate[:], hit[:].rearrange("p (c e) -> p c e", e=NE),
                                    upto[:].rearrange("p (e c) -> p c e", e=NE), ALU.add)
            dve.drain()
            nc.vector.tensor_tensor(gate[:], gate[:], score[:], ALU.mult).then_inc(gate_done, 1)
            for k in range(NT):
                dve.wait_ge(gt_hi, k + 1)
                nc.vector.tensor_tensor(gT_lo[:, k * S:(k + 1) * S], pe_ps[0:NE, k, :], gT_hi[:, k * S:(k + 1) * S].bitcast(F32),
                                        ALU.subtract).then_inc(gt_lo, 1)

            def gated(e, t):
                u = NT * e + t
                dve.wait_ge(down_done, u + 1)
                if isinstance(e, int) and e == 0:
                    nc.vector.tensor_scalar(acc[:, t * S:(t + 1) * S], pe_ps[:, 4 + t % 2, :], b2_sb[:, 0:1], None, ALU.add)\
                      .then_inc(y_done, 1)
                    return
                dve.wait_ge(g_out, u - NT + 1)
                after(dve, acc_done, u - NT - 1)
                nc.vector.scalar_tensor_tensor(part[:, t % 2, :], pe_ps[:, 4 + t % 2, :], b2_sb[:, bass.ds(e, 1)],
                                               gbc[:, t % 2, :], ALU.add, ALU.mult).then_inc(y_done, 1)

            def final(t):
                dve.wait_ge(fin_tr, t + 1)
                rows = res2[:, NC * t:NC * (t + 1), :].rearrange("p c d -> p (c d)")
                nc.vector.tensor_tensor(rows, pe_ps[:, 7, :], x1[:, NC * t:NC * (t + 1), :].rearrange("p c d -> p (c d)"),
                                        ALU.add).then_inc(fin_in, 1)
                dve.drain()
                for c in range(NC * t, NC * (t + 1)):
                    nc.vector.bn_stats(bst2[:, c, :], res2[:, c, :])
                dve.drain()
                for c in range(NC * t, NC * (t + 1)):
                    nc.vector.bn_aggr(bag2[:, c, :], bst2[:, c, :])

            def expert(e, buf):
                for t in range(NT):
                    u = NT * e + t
                    after(dve, down_done, u - 1)
                    for f in range(NF + 1):
                        if f < NF:
                            dve.wait_ge(gelu_done, NF * u + f + 1)
                            nc.vector.tensor_copy(hh[:, t % 2, f, :], h[:, f, :]).then_inc(hh_done, 1)
                        if f > 0:
                            dve.wait_ge(hh_done, NF * u + f)
                            nc.vector.tensor_tensor(hl[:, t % 2, f - 1, :], h[:, f - 1, :],
                                                    hh[:, t % 2, f - 1, :].bitcast(F32), ALU.subtract).then_inc(hl_done, 1)
                    if t > 0:
                        gated(e, t - 1)
                    elif not isinstance(e, int) or e > 0:
                        gated(e - 1, NT - 1)
                    if t == 3 and (not isinstance(e, int) or e < NE):
                        split(e + 1, 1 - buf)
                    if isinstance(e, int) and e == NE and t >= 3:
                        final(t - 3)

            all_experts(nc.vector, expert)
            gated(NE, NT - 1)
            for t in range(NT - 3, NT):
                final(t)
            dve.drain()
            y = rstd(nc, dve, bag2[:, :, 1], nw2)
            for c in range(NCH):
                last = nc.vector.tensor_scalar(res2[:, c, :], res2[:, c, :], bag2[:, c, 0:1], y[:, c:c + 1],
                                               ALU.subtract, ALU.mult)
                if c % NC == NC - 1:
                    last.then_inc(fin_ready, 1)


def rope_tables():
    import numpy as np
    pos = np.arange(S, dtype=np.float32)
    rates = (np.float32(10000.0) ** (-(np.float32(2.0) * np.arange(DK // 2, dtype=np.float32)) / np.float32(DK))).astype(np.float32)
    ang = (pos[:, None] * rates[None, :]).astype(np.float32)
    cos, sin = np.cos(ang).astype(np.float32), np.sin(ang).astype(np.float32)
    row = np.arange(P) // 4 % DK
    sign = np.where(row % 2 == 0, -1.0, 1.0).astype(np.float32)
    return np.ascontiguousarray(cos[:, row // 2].T), np.ascontiguousarray(sin[:, row // 2].T * sign[:, None])


def kernel(**inputs):
    import numpy as np
    import concourse.bacc as bacc
    from concourse.bass_utils import run_bass_kernel_spmd

    x = np.asarray(inputs["L0_attn_x"])
    flat = x.reshape(TOK, D)
    g4, d8, j4 = np.meshgrid(np.arange(NG), np.arange(DK), np.arange(4), indexing="ij")
    dense = ((4 * g4 + j4) * DK + d8).reshape(D)
    other = dense ^ 1
    g = {k: np.asarray(inputs["L0_attn_" + k]) for k in ("Wq", "Wk", "Wv", "Wo")}
    f = {k: np.asarray(inputs["L0_ffn_" + k]) for k in ("gate_weight", "W1", "b1", "W2", "b2", "Ws1", "bs1", "Ws2", "bs2")}
    w1 = np.concatenate([f["Ws1"][None], f["W1"]], 0).transpose(1, 0, 2).reshape(D, NX * F)
    w2 = np.concatenate([f["Ws2"][None], f["W2"]], 0).reshape(NX, NF, P, D).transpose(2, 0, 1, 3).reshape(P, NX * F)
    b1 = np.concatenate([f["bs1"][None], f["b1"]], 0).reshape(NX * NF, P).T
    b2 = np.concatenate([f["bs2"][None], f["b2"]], 0).T
    cos, sin = rope_tables()
    selo = np.zeros((P, 36), np.float32)
    for j in range(4):
        for c in range(9):
            selo[32 * j + c, 9 * j + c] = 1.0
    sele = np.zeros((NE, NE, P), np.float32)
    for e in range(NE):
        sele[e, e] = 1.0
    row = np.arange(P)
    wproj = np.concatenate([g["Wq"][dense].T, g["Wq"][other].T, g["Wk"][dense].T, g["Wk"][other].T, g["Wv"].T], 1)
    heads = (row[:, None] % 4 == np.arange(4)).astype(np.float32)
    minus = -((row >= MROW) & (row < MROW + 8)).astype(np.float32)[:, None]
    parts = dict(wo=g["Wo"].T, gw=f["gate_weight"].T, ident=np.eye(P, dtype=np.float32), selo=selo, heads=heads,
                 minus=minus, b1=b1, b2=b2)
    arrays = dict(
        xT=flat.T, xr=flat, early=np.concatenate([wproj, cos, sin], 1),
        late=np.concatenate([parts[name] for name, _ in LATE], 1), w1=w1, w2=w2, sele=sele.reshape(NE, NE * P),
    )
    arrays = {k: np.ascontiguousarray(v) for k, v in arrays.items()}
    nc = bacc.Bacc("TRN2", target_bir_lowering=False, num_devices=1)
    aps = {k: nc.dram_tensor(k, v.shape, mybir.dt.from_np(v.dtype), kind="ExternalInput").ap() for k, v in arrays.items()}
    out = nc.dram_tensor("y", (TOK, D), F32, kind="ExternalOutput").ap()
    moe_layer(nc, **aps, out=out)
    r = run_bass_kernel_spmd(nc, [arrays], core_ids=[0])
    return r.results[0]["y"].reshape(x.shape)
```
